# Optimizing a Trainium2 kernel written in Bass

```python
import numpy as np
import jax
import jax.numpy as jnp

def _softmax(x, axis=-1):
    return jax.nn.softmax(x, axis=axis)
def _gelu(x):
    return jax.nn.gelu(x, approximate=True)
def _silu(x):
    return jax.nn.silu(x)
def _sigmoid(x):
    return jax.nn.sigmoid(x)
def _layernorm(x, axis=-1, eps=1e-5):
    m = jnp.mean(x, axis=axis, keepdims=True)
    v = jnp.var(x, axis=axis, keepdims=True)
    return (x - m) / jnp.sqrt(v + eps)
def _scatter_add(tgt, idx, src, axis=0):
    return tgt.at[idx].add(src)
def _segment_sum(src, seg, n):
    return jax.ops.segment_sum(src, seg, n)

kernel_name = 'mk_conv_seq_d1_conv_nhwc768_a02469'

def setup_inputs(seed: int = 0):
    np.random.seed(seed)
    _w = jnp.asarray
    def _rec_inputs():
        import jax
        import jax.numpy as jnp
        _gk = jax.random.key(seed)
        x = -4.65e-05 + 0.9999 * jax.random.normal(jax.random.fold_in(_gk, 1), (4, 128, 128, 768), jnp.float32)
        return x
    x = _rec_inputs()
    def _L0_conv_setup():
        import jax, jax.numpy as jnp
        import numpy as np
        NUM_HEADS = 8
        HIDDEN_SIZE = 768
        BLOCK = HIDDEN_SIZE // NUM_HEADS
        FACTOR = 1
        LAMBDA = 0.01
        FRACTION = 1.0
        SCALE = 0.02

        def softshrink(x, lambd):
            return jnp.where(x > lambd, x - lambd, jnp.where(x < -lambd, x + lambd, jnp.zeros_like(x)))
        key = jax.random.key(seed)
        k = jax.random.split(key, 5)
        B, H, W = (4, 128, 128)
        x = jax.random.normal(k[0], (B, H, W, HIDDEN_SIZE), dtype=jnp.float32)
        w1 = SCALE * jax.random.normal(k[1], (2, NUM_HEADS, BLOCK, BLOCK * FACTOR), dtype=jnp.float32)
        b1 = SCALE * jax.random.normal(k[2], (2, NUM_HEADS, BLOCK * FACTOR), dtype=jnp.float32)
        w2 = SCALE * jax.random.normal(k[3], (2, NUM_HEADS, BLOCK * FACTOR, BLOCK), dtype=jnp.float32)
        b2 = SCALE * jax.random.normal(k[4], (2, NUM_HEADS, BLOCK), dtype=jnp.float32)
        return {'x': x, 'w1': w1, 'b1': b1, 'w2': w2, 'b2': b2}
    _L0_conv_all = _L0_conv_setup()
    _L0_conv_in = {k: v for k, v in _L0_conv_all.items() if k in ('w1', 'b1', 'w2', 'b2', )}
    del _L0_conv_all

    return {
        "x": x,
        "L0_conv_w1": _L0_conv_in["w1"],
        "L0_conv_b1": _L0_conv_in["b1"],
        "L0_conv_w2": _L0_conv_in["w2"],
        "L0_conv_b2": _L0_conv_in["b2"],
    }

def reference(x, L0_conv_w1, L0_conv_b1, L0_conv_w2, L0_conv_b2):
    import jax
    import jax.numpy as jnp
    def _L0_conv_ref(x, w1, b1, w2, b2):
        import jax, jax.numpy as jnp
        import numpy as np
        NUM_HEADS = 8
        HIDDEN_SIZE = 768
        BLOCK = HIDDEN_SIZE // NUM_HEADS
        FACTOR = 1
        LAMBDA = 0.01
        FRACTION = 1.0
        SCALE = 0.02

        def softshrink(x, lambd):
            return jnp.where(x > lambd, x - lambd, jnp.where(x < -lambd, x + lambd, jnp.zeros_like(x)))
        bias = x
        dtype = x.dtype
        xf32 = x.astype(jnp.float32)
        B, H, W, C = x.shape
        xs = jnp.fft.rfft2(xf32, axes=(1, 2))
        Wm = W // 2 + 1
        xs = xs.reshape(B, H, Wm, NUM_HEADS, BLOCK)
        total_modes = H // 2 + 1
        kept = int(total_modes * FRACTION)
        lo, hi = (total_modes - kept, min(total_modes + kept, H))
        wk = min(kept, Wm)
        xr = jnp.real(xs[:, lo:hi, :wk])
        xi = jnp.imag(xs[:, lo:hi, :wk])
        o1r = jax.nn.relu(jnp.einsum('bxyhi,hio->bxyho', xr, w1[0]) - jnp.einsum('bxyhi,hio->bxyho', xi, w1[1]) + b1[0])
        o1i = jax.nn.relu(jnp.einsum('bxyhi,hio->bxyho', xi, w1[0]) + jnp.einsum('bxyhi,hio->bxyho', xr, w1[1]) + b1[1])
        o2r = jnp.einsum('bxyho,hoi->bxyhi', o1r, w2[0]) - jnp.einsum('bxyho,hoi->bxyhi', o1i, w2[1]) + b2[0]
        o2i = jnp.einsum('bxyho,hoi->bxyhi', o1i, w2[0]) + jnp.einsum('bxyho,hoi->bxyhi', o1r, w2[1]) + b2[1]
        zr = jnp.zeros((B, H, Wm, NUM_HEADS, BLOCK), dtype=jnp.float32).at[:, lo:hi, :wk].set(o2r)
        zi = jnp.zeros((B, H, Wm, NUM_HEADS, BLOCK), dtype=jnp.float32).at[:, lo:hi, :wk].set(o2i)
        out_c = softshrink(zr, LAMBDA) + 1j * softshrink(zi, LAMBDA)
        out_c = out_c.reshape(B, H, Wm, C)
        out = jnp.fft.irfft2(out_c, s=(H, W), axes=(1, 2))
        return out.astype(dtype) + bias

    def _gn(v, G=32, eps=1e-5):
        B_, H_, W_, C_ = v.shape
        g = v.reshape(B_, H_, W_, G, C_ // G)
        m = jnp.mean(g, axis=(1, 2, 4), keepdims=True)
        s = jnp.var(g, axis=(1, 2, 4), keepdims=True)
        return ((g - m) / jnp.sqrt(s + eps)).reshape(v.shape)

    def _ln_c(v, eps=1e-6):
        m = jnp.mean(v, axis=-1, keepdims=True)
        s = jnp.var(v, axis=-1, keepdims=True)
        return (v - m) / jnp.sqrt(s + eps)

    def _ln_t(v, eps=1e-5):
        m = jnp.mean(v, axis=-1, keepdims=True)
        s = jnp.var(v, axis=-1, keepdims=True)
        return (v - m) / jnp.sqrt(s + eps)

    def _to_tokens(v):
        B_, H_, W_, C_ = v.shape
        return v.reshape(B_, H_ * W_, C_)
    def _from_tokens(t, like):
        return t.reshape(like.shape)

    x = _L0_conv_ref(x, L0_conv_w1, L0_conv_b1, L0_conv_w2, L0_conv_b2)
    return x


_drawn_inputs = setup_inputs


def setup_inputs(seed=0):
    import zlib

    import numpy as np

    out = dict(_drawn_inputs(seed))
    spreads = {}
    factors = {'L0_conv_b1': 200.0, 'L0_conv_b2': 200.0}
    for name, (base, spread) in spreads.items():
        noise = np.random.default_rng([zlib.crc32(name.encode()), seed]).standard_normal(out[name].shape)
        drawn = base * np.exp(spread * noise) if base else spread * noise
        out[name] = jnp.asarray(drawn.astype(out[name].dtype))
    for name, factor in factors.items():
        out[name] = (out[name] * factor).astype(out[name].dtype)
    return out
```

```python
import concourse.bass as bass
from concourse import mybir
from contextlib import ExitStack


def fourier_mixer_kernel(nc, x, w1, b1, w2, b2, f_w, f_h, g_h, g_w, mirror, turn, out):
    F32 = mybir.dt.float32
    ALU = mybir.AluOpType
    ACT = mybir.ActivationFunctionType

    IMAGES, H, W, CHANNELS = x.shape
    HEADS, C = w1.shape[1], w1.shape[2]
    P = 128
    assert H == W == P
    HALF = P // 2
    LAMBDA = 0.01
    NCOS, NSIN = HALF + 1, HALF - 1

    GC = 4
    GROUPS = C // GC
    A_BANKS = 4
    CK = 4
    CHUNKS = [[0, HALF]] + [list(range(k, min(k + CK, HALF))) for k in range(1, HALF, CK)]
    NCH = len(CHUNKS)
    DK = 2
    MERGED = 1
    BANKS_OF = [[(0, 0, DK)]]
    for ks in CHUNKS[1:]:
        BANKS_OF.append([(1 + sum(map(len, BANKS_OF)) + i, k, min(DK, len(ks) - k))
                         for i, k in enumerate(range(0, len(ks), DK))])
    NB = 1 + sum(map(len, BANKS_OF))
    assert NB % 2 == 0
    LOADS = 4
    HL = H // LOADS
    PAIRS = HEADS // 2

    with ExitStack() as ctx:
        def sb(name, shape, dt=F32):
            return ctx.enter_context(nc.sbuf_tensor(name, shape, dt))

        def sem(name):
            return ctx.enter_context(nc.semaphore(name))

        tile = [sb(f"tile{s}", [P, H, C]) for s in range(2)]
        spec = sb("spec", [P, P + HALF, C])
        real_z = sb("real_z", [P, 2, 2, C])
        xr = [sb(f"xr{i}", [C, CK, P]) for i in range(2)]
        xi = [sb(f"xi{i}", [C, CK, P]) for i in range(2)]
        o_r = [sb(f"o_r{i}", [C + 1, CK, P]) for i in range(2)]
        o_i = [sb(f"o_i{i}", [C, CK, P]) for i in range(2)]
        above = [sb(f"above{i}", [P, 2, DK * C]) for i in range(2)]
        u = [sb(f"u{i}", [P, GC, H]) for i in range(2)]
        w1t = [sb(f"w1t{s}", [C, 3, C]) for s in range(2)]
        w2a = [sb(f"w2a{s}", [C + 1, 2, C]) for s in range(2)]
        w2b = [sb(f"w2b{s}", [C, 2, C]) for s in range(2)]
        b1t = [sb(f"b1t{s}", [C, 2]) for s in range(2)]
        fw = sb("fw", [P, P])
        fh = sb("fh", [P, P])
        gh = sb("gh", [P, P])
        gw = sb("gw", [P, P])
        mir = sb("mir", [P, 3, P])
        sgn = sb("sgn", [P, 2])
        low = sb("low", [P, 1])
        minus = sb("minus", [C, C])
        started = sb("started", [P, 1])
        ones = sb("ones", [P, DK + 1, C])

        bank = [ctx.enter_context(nc.psum_tensor(f"bank{i}", [P, 512], F32)) for i in range(8)]
        b_bank = bank[0:4]
        c_bank = bank[4:6]
        d_bank = bank[6:8]

        consts_in = sem("consts_in")
        set_once = sem("set_once")
        x_loaded = [sem(f"x_loaded{s}") for s in range(2)]
        x_stored = [sem(f"x_stored{s}") for s in range(2)]
        w_loaded = [sem(f"w_loaded{s}") for s in range(2)]
        w_ready = [sem(f"w_ready{s}") for s in range(2)]
        a_done = sem("a_done")
        y_ready = sem("y_ready")
        b_done = sem("b_done")
        b_copied = sem("b_copied")
        x_ready = sem("x_ready")
        c_done = sem("c_done")
        o_ready = sem("o_ready")
        d_done = sem("d_done")
        above_ready = sem("above_ready")
        z_ready = sem("z_ready")
        z_doubled = sem("z_doubled")
        e_done = sem("e_done")
        e_copied = sem("e_copied")
        u_ready = sem("u_ready")
        f_done = sem("f_done")
        added = sem("added")

        x_v = x.rearrange("b h w (g s c) -> b g s w h c", s=2, c=C)
        out_v = out.rearrange("b h w (g s c) -> b g s w h c", s=2, c=C)
        w1_v = w1.rearrange("r (g s) i o -> g s i r o", s=2)
        b1_v = b1.rearrange("r (g s) o -> g s o r", s=2)
        w2_v = w2.rearrange("r (g s) i o -> g s r i o", s=2)
        b2_v = b2.rearrange("r (g s) (a o) -> g s a r o", s=2, a=1)
        W_DMAS = 6

        block = ctx.enter_context(nc.Block())

        @block.sync
        def _(sp):
            for dst, src in ((fw, f_w), (fh, f_h), (gh, g_h), (gw, g_w), (mir, mirror), (sgn, turn)):
                sp.dma_start(dst[:], src).then_inc(consts_in, 16)
            with sp.Fori(0, IMAGES) as b:
                with sp.Fori(0, PAIRS) as g:
                    t = b * PAIRS + g
                    for s in range(2):
                        sp.wait_ge(x_stored[s], t * (16 * LOADS) + 1)
                        for q in range(LOADS):
                            sp.dma_start(tile[s][:, q * HL:(q + 1) * HL, :],
                                         x_v[b, g, s, :, q * HL:(q + 1) * HL, :]).then_inc(x_loaded[s], 16)
                        sp.dma_start(w1t[s][:, 0:2, :], w1_v[g, s]).then_inc(w_loaded[s], 16)
                        sp.dma_start(b1t[s][:], b1_v[g, s], allow_slow_non_contiguous=True).then_inc(w_loaded[s], 16)
                        for r in range(2):
                            sp.dma_start(w2a[s][0:C, r, :], w2_v[g, s, r]).then_inc(w_loaded[s], 16)
                        sp.dma_start(w2b[s][:, 1, :], w2_v[g, s, 0]).then_inc(w_loaded[s], 16)
                        sp.dma_start(w2a[s][C:C + 1, :, :], b2_v[g, s]).then_inc(w_loaded[s], 16)

        @block.gpsimd
        def _(pool):
            nc.gpsimd.memset(low[:], -LAMBDA)
            nc.gpsimd.memset(minus[:], -1.0)
            nc.gpsimd.memset(ones[:], 1.0).then_inc(set_once, 1)
            pool.wait_ge(set_once, 1)
            with pool.Fori(0, IMAGES * PAIRS) as t:
                for s in range(2):
                    pool.wait_ge(w_loaded[s], (t + 1) * (16 * W_DMAS))
                    nc.gpsimd.tensor_tensor(w1t[s][:, 2, :], w1t[s][:, 1, :], minus[:], ALU.mult)
                    nc.gpsimd.tensor_tensor(w2b[s][:, 0, :], w2a[s][0:C, 1, :], minus[:],
                                            ALU.mult).then_inc(w_ready[s], 1)
                    for k in range(1, NCH):
                        for j, k0, m in BANKS_OF[k]:
                            ky = CHUNKS[k][k0]
                            if j == MERGED + 1:
                                ky, m = 0, m + 1
                            pool.wait_ge(z_ready, (t * 2 + s) * NB + (j + 1))
                            real = spec[:, ky:ky + m, :]
                            last = nc.gpsimd.tensor_tensor(spec[:, P + ky:P + ky + m, :], real,
                                                           ones[:, 0:m, :], ALU.mult)
                    last.then_inc(z_doubled, 1)

        @block.tensor
        def _(pe):
            def stage_a(n, s):
                for g in range(GROUPS):
                    if g >= A_BANKS:
                        pe.wait_ge(y_ready, n * GROUPS + (g - A_BANKS + 1))
                    for c in range(GC):
                        last = nc.tensor.matmul(b_bank[g % A_BANKS][:, c * P:(c + 1) * P],
                                                tile[s][:, :, g * GC + c], fw[:], start=True, stop=True)
                    last.then_inc(a_done, 1)

            def stage_b(n, s, k):
                if k == 0:
                    pe.wait_ge(y_ready, (n + 1) * GROUPS)
                if k >= 2:
                    pe.wait_ge(x_ready, n * NCH + (k - 1))
                re, im = b_bank[2 * (k % 2)], b_bank[2 * (k % 2) + 1]
                for i, ky in enumerate(CHUNKS[k]):
                    last = nc.tensor.matmul(re[0:C, i * P:(i + 1) * P], spec[:, ky, :], fh[:],
                                            start=True, stop=True)
                    if k:
                        last = nc.tensor.matmul(im[0:C, i * P:(i + 1) * P], spec[:, HALF + ky, :], fh[:],
                                                start=True, stop=True)
                last.then_inc(b_done, 1)

            def stage_c(n, s, k):
                pe.wait_ge(x_ready, n * NCH + (k + 1))
                if k:
                    pe.wait_ge(o_ready, n * NCH + k)
                m = len(CHUNKS[k])
                r, i = xr[k % 2][:, 0:m, :], xi[k % 2][:, 0:m, :]
                W1 = w1t[s]
                for o, (a, b) in zip(c_bank, (((0, r), (2, i)), ((0, i), (1, r)))):
                    nc.tensor.matmul(o[0:C, 0:m * P], W1[:, a[0], :], a[1], start=True, stop=False)
                    last = nc.tensor.matmul(o[0:C, 0:m * P], W1[:, b[0], :], b[1], start=False, stop=True)
                last.then_inc(c_done, 1)

            def stage_d(n, s, k):
                pe.wait_ge(o_ready, n * NCH + (k + 1))
                for j, k0, m in BANKS_OF[k]:
                    if j >= 2:
                        pe.wait_ge(z_ready, n * NB + (j - 1))
                    else:
                        pe.wait_ge(added, n * GROUPS + 1)
                    o = d_bank[j % 2][:, 0:2 * m * C].rearrange("p (r k c) -> p k r c", r=2, c=C)
                    for i in range(m):
                        nc.tensor.matmul(o[:, i], o_r[k % 2][:, k0 + i, :], w2a[s][:], start=True, stop=False)
                        last = nc.tensor.matmul(o[:, i], o_i[k % 2][:, k0 + i, :], w2b[s][:],
                                                start=False, stop=True)
                    last.then_inc(d_done, 1)

            def merge_real(n):
                pe.wait_ge(z_ready, n * NB + 1)
                o = d_bank[MERGED % 2]
                pe.wait_ge(added, n * GROUPS + 1)
                even, odd, minus_odd = mir[:, 0, :], mir[:, 1, :], mir[:, 2, :]
                nc.tensor.matmul(o[:, 0:C], even, real_z[:, 0, 0, :], start=True, stop=False)
                nc.tensor.matmul(o[:, 0:C], minus_odd, real_z[:, 1, 1, :], start=False, stop=True)
                nc.tensor.matmul(o[:, C:2 * C], even, real_z[:, 0, 1, :], start=True, stop=False)
                nc.tensor.matmul(o[:, C:2 * C], odd, real_z[:, 1, 0, :], start=False,
                                 stop=True).then_inc(d_done, 1)

            def stage_e(n, g):
                if g == 0:
                    pe.wait_ge(z_ready, (n + 1) * NB)
                    pe.wait_ge(z_doubled, n + 1)
                if g >= 2:
                    pe.wait_ge(u_ready, n * GROUPS + (g - 1))
                o = c_bank[g % 2][:, :].rearrange("p (c h) -> p c h", c=GC)
                for c in range(GC):
                    nc.tensor.matmul(o[:, c, 0:NCOS], spec[:, 0:P, g * GC + c], gh[:, 0:NCOS],
                                     start=True, stop=True)
                    last = nc.tensor.matmul(o[:, c, NCOS:P], spec[:, HALF:, g * GC + c], gh[:, NCOS:P],
                                            start=True, stop=True)
                last.then_inc(e_done, 1)

            def stage_f(n, g):
                pe.wait_ge(u_ready, n * GROUPS + (g + 1))
                if g >= 2:
                    pe.wait_ge(added, n * GROUPS + g)
                nc.tensor.matmul(d_bank[g % 2][:, :], gw[:], u[g % 2][:], start=True,
                                 stop=True).then_inc(f_done, 1)

            pe.wait_ge(consts_in, 16 * 6)
            pe.wait_ge(added, 1)
            with pe.Fori(0, IMAGES * PAIRS) as t:
                for s in range(2):
                    n = t * 2 + s
                    pe.wait_ge(x_loaded[s], (t + 1) * (16 * LOADS))
                    stage_a(n, s)
                    pe.wait_ge(w_ready[s], t + 1)
                    for k in range(-2, NCH):
                        if k + 2 < NCH:
                            stage_b(n, s, k + 2)
                        if 0 <= k + 1 < NCH:
                            stage_c(n, s, k + 1)
                        if k == 1:
                            merge_real(n)
                        if k >= 0:
                            stage_d(n, s, k)
                    for g in range(-2, GROUPS):
                        if g >= 0:
                            stage_f(n, g)
                        if g + 2 < GROUPS:
                            stage_e(n, g + 2)

        @block.scalar
        def _(act):
            def copy_y(n, g):
                act.wait_ge(a_done, n * GROUPS + (g + 1))
                nc.scalar.activation(spec[:, 0:P, g * GC:(g + 1) * GC].rearrange("p k c -> p c k"),
                                     b_bank[g % A_BANKS][:, :].rearrange("p (c k) -> p c k", c=GC),
                                     ACT.Copy).then_inc(y_ready, 1)

            def copy_b(n, k):
                act.wait_ge(b_done, n * NCH + (k + 1))
                m = len(CHUNKS[k])
                r, i = xr[k % 2][:, 0:m, :], xi[k % 2][:, 0:m, :]
                re, im = (b_bank[2 * (k % 2) + j][0:C, 0:m * P].rearrange("c (k m) -> c k m", k=m)
                          for j in range(2))
                nc.scalar.activation(r[:, :, 0:NCOS], re[:, :, 0:NCOS], ACT.Copy)
                if k:
                    nc.scalar.activation(i[:, :, 0:NCOS], im[:, :, 0:NCOS], ACT.Copy).then_inc(b_copied, 1)
                else:
                    nc.scalar.activation(r[:, :, NCOS:P], re[:, :, 1:HALF], ACT.Copy)
                    nc.scalar.activation(i[:, :, NCOS:P], re[:, :, NCOS:P], ACT.Copy).then_inc(b_copied, 1)

            def relu(n, s, k):
                act.wait_ge(c_done, n * NCH + (k + 1))
                m = len(CHUNKS[k])
                for j, o in enumerate((o_r, o_i)):
                    last = nc.scalar.activation(o[k % 2][0:C, 0:m, :], c_bank[j][0:C, 0:m * P], ACT.Relu,
                                                bias=b1t[s][:, j:j + 1])
                last.then_inc(o_ready, 1)

            def shrink_above(n, k):
                for j, _, m in BANKS_OF[k]:
                    act.wait_ge(d_done, n * NB + (j + 1))
                    nc.scalar.activation(above[j % 2][:, :, 0:m * C], d_bank[j % 2][:, 0:2 * m * C], ACT.Relu,
                                         bias=low[:]).then_inc(above_ready, 1)

            def copy_e(n, g):
                act.wait_ge(e_done, n * GROUPS + (g + 1))
                if g >= 2:
                    act.wait_ge(f_done, n * GROUPS + (g - 1))
                nc.scalar.activation(u[g % 2][:, :, 0:NCOS],
                                     c_bank[g % 2][:, :].rearrange("p (c h) -> p c h", c=GC)[:, :, 0:NCOS],
                                     ACT.Copy).then_inc(e_copied, 1)

            act.wait_ge(set_once, 1)
            with act.Fori(0, IMAGES) as b:
                with act.Fori(0, PAIRS) as p:
                    t = b * PAIRS + p
                    for s in range(2):
                        n = t * 2 + s
                        for g in range(GROUPS):
                            copy_y(n, g)
                        act.wait_ge(w_loaded[s], (t + 1) * (16 * W_DMAS))
                        for k in range(-2, NCH):
                            if k + 2 < NCH:
                                copy_b(n, k + 2)
                            if 0 <= k + 1 < NCH:
                                relu(n, s, k + 1)
                            if k >= 0:
                                shrink_above(n, k)
                        for g in range(GROUPS):
                            copy_e(n, g)
                        act.wait_ge(added, (n + 1) * GROUPS + 1)
                        for q in range(LOADS):
                            act.dma_start(out_v[b, p, s, :, q * HL:(q + 1) * HL, :],
                                          tile[s][:, q * HL:(q + 1) * HL, :]).then_inc(x_stored[s], 16)
            for s in range(2):
                act.wait_ge(x_stored[s], 16 * LOADS * IMAGES * PAIRS + 1)

        @block.vector
        def _(dve):
            def combine_b(n, k):
                dve.wait_ge(b_copied, n * NCH + (k + 1))
                m = len(CHUNKS[k])
                r, i = xr[k % 2][:, 0:m, :], xi[k % 2][:, 0:m, :]
                re, im = (b_bank[2 * (k % 2) + j][0:C, 0:m * P].rearrange("c (k m) -> c k m", k=m)
                          for j in range(2))
                plus, minus, sin = slice(1, HALF), slice(NCOS, P), slice(NCOS, P)
                if k == 0:
                    nc.vector.memset(i[:, :, 0:NCOS:HALF], 0.0)
                    nc.vector.tensor_scalar(i[:, :, plus], re[:, :, sin], -1.0, None,
                                            ALU.mult).then_inc(x_ready, 1)
                    return
                nc.vector.tensor_tensor(r[:, :, minus], r[:, :, plus], im[:, :, sin], ALU.subtract)
                nc.vector.tensor_tensor(i[:, :, minus], i[:, :, plus], re[:, :, sin], ALU.add)
                nc.vector.tensor_tensor(r[:, :, plus], r[:, :, plus], im[:, :, sin], ALU.add)
                nc.vector.tensor_tensor(i[:, :, plus], i[:, :, plus], re[:, :, sin],
                                        ALU.subtract).then_inc(x_ready, 1)

            def shrink(n, k):
                for i, (j, k0, m) in enumerate(BANKS_OF[k]):
                    dve.wait_ge(above_ready, n * (NB - 1) + (j + 1 if j == 0 else j))
                    if k == 0:
                        dst = real_z[:, :, :, :].rearrange("p r k c -> p r (k c)")
                    else:
                        ky = CHUNKS[k][k0]
                        dst = spec[:, 0:P, :].rearrange("p (r k) c -> p r (k c)", r=2)[:, :, ky * C:(ky + m) * C]
                    nc.vector.scalar_tensor_tensor(
                        dst, d_bank[j % 2][:, 0:2 * m * C].rearrange("p (r c) -> p r c", r=2), LAMBDA,
                        above[j % 2][:, :, 0:m * C], ALU.add, ALU.min).then_inc(z_ready, 1)

            def copy_merged(n):
                dve.wait_ge(d_done, n * NB + (MERGED + 1))
                nc.vector.tensor_copy(spec[:, 0:P:HALF, :],
                                      d_bank[MERGED % 2][:, 0:2 * C].rearrange("p (r c) -> p r c", r=2)
                                      ).then_inc(z_ready, 1)

            def combine_e(n, g):
                dve.wait_ge(e_copied, n * GROUPS + (g + 1))
                o = u[g % 2]
                sin = c_bank[g % 2][:, :].rearrange("p (c h) -> p c h", c=GC)[:, :, NCOS:P]
                nc.vector.scalar_tensor_tensor(o[:, :, P - 1:HALF:-1], sin, sgn[:, 1:2], o[:, :, 1:HALF],
                                               ALU.mult, ALU.add)
                nc.vector.scalar_tensor_tensor(o[:, :, 1:HALF], sin, sgn[:, 0:1], o[:, :, 1:HALF],
                                               ALU.mult, ALU.add).then_inc(u_ready, 1)

            def add_x(n, s, g):
                dve.wait_ge(f_done, n * GROUPS + (g + 1))
                dst = tile[s][:, :, g * GC:(g + 1) * GC].rearrange("p h c -> p c h")
                nc.vector.tensor_tensor(dst, dst, d_bank[g % 2][:, :].rearrange("p (c h) -> p c h", c=GC),
                                        ALU.add).then_inc(added, 1)

            for i in range(2):
                nc.vector.memset(o_r[i][C:C + 1, :, :], 1.0).then_inc(x_stored[i], 1)
            nc.vector.memset(started[:], 0.0).then_inc(added, 1)
            dve.wait_ge(consts_in, 16 * 6)
            with dve.Fori(0, IMAGES * PAIRS) as t:
                for s in range(2):
                    n = t * 2 + s
                    for k in range(-2, NCH):
                        if k + 2 < NCH:
                            combine_b(n, k + 2)
                        if k == 1:
                            copy_merged(n)
                        if k >= 0:
                            shrink(n, k)
                    for g in range(-2, GROUPS):
                        if g >= 0:
                            add_x(n, s, g)
                        if g + 2 < GROUPS:
                            combine_e(n, g + 2)


_INS = ["x", "L0_conv_w1", "L0_conv_b1", "L0_conv_w2", "L0_conv_b2"]


def _tables(p):
    import numpy as np
    half = p // 2
    angle = 2 * np.pi * (np.outer(np.arange(p), np.arange(half + 1)) % p) / p
    cos, sin = np.cos(angle), np.sin(angle)
    kx = np.concatenate([np.arange(half + 1), -np.arange(1, half)])
    f_w = np.concatenate([cos[:, :half + 1], -sin[:, 1:half]], 1)
    f_h = np.concatenate([cos, sin[:, 1:half]], 1)
    back = 2 * np.pi * (np.outer(kx, np.arange(half + 1)) % p) / p
    g_h = np.concatenate([np.cos(back), np.sin(back)[:, 1:half]], 1)
    g_w = 2 * f_w.T / p ** 2
    g_w[0] /= 2
    g_w[half] /= 2
    partner = np.array([list(kx % p).index((-k) % p) for k in kx])
    same, swap = np.eye(p), np.eye(p)[partner]
    even, odd = (same + swap) / 2, (same - swap) / 2
    mirror = np.stack([even, odd.T, -odd.T], 1)
    turn = np.ones((p, 2))
    turn[:half, 0] = -1
    turn[half:, 1] = -1
    return {k: np.ascontiguousarray(v, np.float32) for k, v in
            dict(f_w=f_w, f_h=f_h, g_h=g_h, g_w=g_w, mirror=mirror, turn=turn).items()}


def kernel(**inputs):
    import numpy as _np
    import concourse.bacc as _bacc
    from concourse import mybir as _mybir
    from concourse.bass_utils import run_bass_kernel_spmd as _run

    nc = _bacc.Bacc("TRN2", target_bir_lowering=False, num_devices=1)
    arrays, args = {}, []
    for name in _INS:
        arrays[f"in_{name}_dram"] = _np.ascontiguousarray(inputs[name])
    for name, a in _tables(128).items():
        arrays[f"const_{name}_dram"] = a
    for name, a in arrays.items():
        args.append(nc.dram_tensor(name, a.shape, _mybir.dt.from_np(a.dtype), kind="ExternalInput").ap())
    shape = inputs["x"].shape
    args.append(nc.dram_tensor("out_0_dram", shape, _mybir.dt.float32, kind="ExternalOutput").ap())
    fourier_mixer_kernel(nc, *args)
    r = _run(nc, [arrays], core_ids=[0])
    return r.results[0]["out_0_dram"]
```

```python
import concourse.bass as bass
from concourse import mybir
from contextlib import ExitStack


def fourier_mixer_kernel(nc, x, w1, b1, w2, b2, f_x, g_h_high, g_h_rest, g_w, mirror, turn,
                         chunk_of_slot, diagonal, out):
    F32, F32R, F16, BF16 = mybir.dt.float32, mybir.dt.float32r, mybir.dt.float16, mybir.dt.bfloat16
    I32 = mybir.dt.int32
    ALU = mybir.AluOpType
    ACT = mybir.ActivationFunctionType
    AX = mybir.AxisListType

    IMAGES, H, W, CHANNELS = x.shape
    HEADS, C = w1.shape[1], w1.shape[2]
    P = 128
    assert H == W == P
    HALF = P // 2
    LAMBDA = 0.01
    LEAST = 1e-30
    NCOS, NSIN = HALF + 1, HALF - 1

    GC = 4
    GROUPS = C // GC
    A_BANKS = 4
    CK = 4
    CHUNKS = [[0, HALF]] + [list(range(k, min(k + CK, HALF))) for k in range(1, HALF, CK)]
    NCH = len(CHUNKS)
    DK = 2
    MERGED = 1
    BANKS_OF = [[(0, 0, DK)]]
    for ks in CHUNKS[1:]:
        BANKS_OF.append([(1 + sum(map(len, BANKS_OF)) + i, k, min(DK, len(ks) - k))
                         for i, k in enumerate(range(0, len(ks), DK))])
    NB = 1 + sum(map(len, BANKS_OF))
    assert NB % 2 == 0
    NS = NCH
    LATE = NCH - 2
    SHARED_EXPONENT = 14
    EXPONENT_MASK = 0x7F800000
    SCALE_BITS = (2 * 127 + SHARED_EXPONENT) << 23
    E_BANKS = 4
    LOADS = 4
    HL = H // LOADS
    PAIRS = HEADS // 2

    with ExitStack() as ctx:
        def sb(name, shape, dt=F32):
            return ctx.enter_context(nc.sbuf_tensor(name, shape, dt))

        def sem(name):
            return ctx.enter_context(nc.semaphore(name))

        tile = [sb(f"tile{s}", [P, H, C]) for s in range(2)]
        spec = sb("spec", [P, P + HALF, C])
        zs = sb("zs", [P, 1 + 2 * CK * C])
        real_zs = sb("real_zs", [P, 1 + 2 * 2 * C])
        real_z = real_zs[:, 1:].rearrange("p (r k c) -> p r k c", r=2, c=C)
        xs_u = sb("xs_u", [P, 2, CK * P])
        late_zs = xs_u[:, :, :].rearrange("p r k -> p (r k)")
        xs = xs_u[0:C, :, :].rearrange("c r (k m) -> c r k m", m=P)
        high = [sb(f"high{i}", [P, 2, CK * P], F32R) for i in range(2)]
        rest = [sb(f"rest{i}", [P, 2, CK * P], F32R) for i in range(2)]
        o_r = [sb(f"o_r{i}", [C + 1, CK, P]) for i in range(2)]
        o_u = [sb(f"o_u{i}", [P, CK * P]) for i in range(2)]
        o_i = [o[0:C, :].rearrange("c (k m) -> c k m", m=P) for o in o_u]
        us = [o_u[0][:, :], o_u[1][:, :], xs_u[:, 0, :], xs_u[:, 1, :]]
        us = [v.rearrange("p (c h) -> p c h", c=GC) for v in us]
        w1t = real_zs[0:C, 1:1 + 2 * C].rearrange("c (r o) -> c r o", r=2)
        w1_high = sb("w1_high", [C, 3, C], F32R)
        w1_rest = sb("w1_rest", [C, 3, C], F32R)
        w2t = sb("w2t", [C + 1, 3, C])
        b1t = sb("b1t", [C, 2])
        fx = sb("fx", [P, P])
        gh_high = sb("gh_high", [P, P], F16)
        gh_rest = sb("gh_rest", [P, P], F16)
        gw = real_zs[:, 1:1 + P]
        gw_high = sb("gw_high", [P, P], F32R)
        gw_rest = sb("gw_rest", [P, P], F32R)
        mir = sb("mir", [P, 2, P])
        single = sb("single", [P, 10])
        low = single[:, 0:1]
        one = single[:, 1:2]
        started = single[:, 3:5]
        back = single[:, 5:6]
        sgn = single[:, 6:8]
        turned = single[:, 8:10]
        scales = sb("scales", [P, 4, NS])
        largest = scales[:, 0, :]
        top = scales[:, 1, :]
        power = scales[:, 2, :]
        scale = scales[:, 3, :]
        own = sb("own", [NS, NS], BF16)
        pick = sb("pick", [NS, P], BF16)
        picks = real_zs[0:NS, 1 + P:1 + 2 * P]
        diag = sb("diag", [NS, NS])

        psum = ctx.enter_context(nc.psum_tensor("banks", [P, 8, 512], F32))
        b_bank = [psum[:, i, :] for i in range(4)]
        c_bank = [psum[:, 4 + i, :] for i in range(2)]
        d_bank = [psum[:, 6 + i, :] for i in range(2)]
        e_bank = b_bank
        slot_scales = c_bank[0][:, 0:NS]

        consts_in = sem("consts_in")
        set_once = sem("set_once")
        x_loaded = [sem(f"x_loaded{s}") for s in range(2)]
        x_stored = [sem(f"x_stored{s}") for s in range(2)]
        w1_loaded = sem("w1_loaded")
        w2_loaded = sem("w2_loaded")
        w_high = sem("w_high")
        w_ready = sem("w_ready")
        g_high = sem("g_high")
        g_ready = sem("g_ready")
        a_done = sem("a_done")
        y_ready = sem("y_ready")
        b_done = sem("b_done")
        b_copied = sem("b_copied")
        combined = sem("combined")
        x_high = sem("x_high")
        x_ready = sem("x_ready")
        c_done = sem("c_done")
        o_ready = sem("o_ready")
        d_done = sem("d_done")
        above_ready = sem("above_ready")
        z_ready = sem("z_ready")
        turned_real = sem("turned_real")
        largest_ready = sem("largest_ready")
        top_ready = sem("top_ready")
        power_ready = sem("power_ready")
        scale_ready = sem("scale_ready")
        z_high = sem("z_high")
        z_split = sem("z_split")
        z_doubled = sem("z_doubled")
        own_ready = sem("own_ready")
        picked = sem("picked")
        back_ready = sem("back_ready")
        turned_ready = sem("turned_ready")
        e_done = sem("e_done")
        e_copied = sem("e_copied")
        combined_u = sem("combined_u")
        u_high = sem("u_high")
        u_ready = sem("u_ready")
        f_done = sem("f_done")
        added = sem("added")

        x_v = x.rearrange("b h w (g s c) -> b g s w h c", s=2, c=C)
        out_v = out.rearrange("b h w (g s c) -> b g s w h c", s=2, c=C)
        w1_v = w1.rearrange("r (g s) i o -> g s i r o", s=2)
        b1_v = b1.rearrange("r (g s) o -> g s o r", s=2)
        w2_v = w2.rearrange("r (g s) i o -> g s r i o", s=2)
        b2_v = b2.rearrange("r (g s) (a o) -> g s a r o", s=2, a=1)
        W2_DMAS = 4
        CONSTANTS = 8

        def parts(j, m):
            return d_bank[j % 2][:, 0:2 * m * C].rearrange("p (r c) -> p r c", r=2)

        def z_place(k, k0, m):
            if k == 0:
                return real_z.rearrange("p r k c -> p r (k c)")
            return unscaled(k)[0][:, :, k0 * C:(k0 + m) * C]

        def unscaled(i):
            m = len(CHUNKS[i]) if i else 1
            row = (late_zs if i == NCH - 2 else zs if i else real_zs)[:, 0:1 + 2 * m * C]
            return row[:, 1:].rearrange("p (r c) -> p r c", r=2), row

        z_parts = spec[:, :, :].bitcast(F16).rearrange("p k (q c) -> p k q c", q=2)

        def z_slots(i, part):
            ky, m = (CHUNKS[i][0], len(CHUNKS[i])) if i else (0, 1)
            return z_parts[:, 0:P, part, :].rearrange("p (r k) c -> p r k c", r=2)[:, :, ky:ky + m, :]

        block = ctx.enter_context(nc.Block())

        @block.sync
        def _(sp):
            for dst, src in ((fx[:], f_x), (gh_high[:], g_h_high), (gh_rest[:], g_h_rest),
                             (gw, g_w), (mir[:], mirror), (sgn, turn), (picks, chunk_of_slot),
                             (diag[:], diagonal)):
                sp.dma_start(dst, src).then_inc(consts_in, 16)
            with sp.Fori(0, IMAGES) as b:
                with sp.Fori(0, PAIRS) as g:
                    t = b * PAIRS + g
                    for s in range(2):
                        n = t * 2 + s
                        sp.wait_ge(x_stored[s], t * (16 * LOADS) + 1)
                        for q in range(LOADS):
                            sp.dma_start(tile[s][:, q * HL:(q + 1) * HL, :],
                                         x_v[b, g, s, :, q * HL:(q + 1) * HL, :]).then_inc(x_loaded[s], 16)
                        sp.wait_ge(turned_ready, n + 1)
                        sp.dma_start(w1t, w1_v[g, s]).then_inc(w1_loaded, 16)
                        sp.dma_start(b1t[:], b1_v[g, s], allow_slow_non_contiguous=True).then_inc(w2_loaded, 16)
                        for r in range(2):
                            sp.dma_start(w2t[0:C, 1 + r, :], w2_v[g, s, r]).then_inc(w2_loaded, 16)
                        sp.dma_start(w2t[C:C + 1, 1:3, :], b2_v[g, s]).then_inc(w2_loaded, 16)

        @block.gpsimd
        def _(pool):
            nc.gpsimd.memset(low, -LAMBDA)
            nc.gpsimd.memset(one, 1.0)
            nc.gpsimd.memset(zs[:, 0:1], LEAST)
            nc.gpsimd.memset(real_zs[:, 0:1], LEAST).then_inc(set_once, 1)
            pool.wait_ge(set_once, 1)

            def find_top(n, i):
                pool.wait_ge(largest_ready, n * NS + (i + 1))
                nc.gpsimd.tensor_tensor(scale[:, i:i + 1], one, one, ALU.mult)
                nc.gpsimd.partition_all_reduce(top[:, i:i + 1], largest[:, i:i + 1], P,
                                               bass.bass_isa.ReduceOp.max).then_inc(top_ready, 1)

            def rest_u(n, g):
                q = g % E_BANKS
                pool.wait_ge(u_high, n * GROUPS + (g + 1))
                nc.gpsimd.tensor_tensor(rest[q % 2][:, q // 2, :], us[q].rearrange("p c h -> p (c h)"),
                                        high[q % 2][:, q // 2, :].bitcast(F32),
                                        ALU.subtract).then_inc(u_ready, 1)

            with pool.Fori(0, IMAGES * PAIRS) as t:
                for s in range(2):
                    n = t * 2 + s
                    for i in range(NS):
                        find_top(n, i)
                    for g in range(GROUPS):
                        rest_u(n, g)

        @block.tensor
        def _(pe):
            def stage_a(n, s):
                for g in range(GROUPS):
                    if g >= A_BANKS:
                        pe.wait_ge(y_ready, n * GROUPS + (g - A_BANKS + 1))
                    for c in range(GC):
                        last = nc.tensor.matmul(b_bank[g % A_BANKS][:, c * P:(c + 1) * P],
                                                tile[s][:, :, g * GC + c], fx[:], start=True, stop=True)
                    last.then_inc(a_done, 1)

            def stage_b(n, s, k):
                if k == 0:
                    pe.wait_ge(y_ready, (n + 1) * GROUPS)
                if k >= 2:
                    pe.wait_ge(combined, n * NCH + (k - 1))
                re, im = b_bank[2 * (k % 2)], b_bank[2 * (k % 2) + 1]
                for i, ky in enumerate(CHUNKS[k]):
                    last = nc.tensor.matmul(re[0:C, i * P:(i + 1) * P], spec[:, ky, :], fx[:],
                                            start=True, stop=True)
                    if k:
                        last = nc.tensor.matmul(im[0:C, i * P:(i + 1) * P], spec[:, HALF + ky, :], fx[:],
                                                start=True, stop=True)
                last.then_inc(b_done, 1)

            def stage_c(n, s, k):
                pe.wait_ge(x_ready, n * NCH + (k + 1))
                if k:
                    pe.wait_ge(o_ready, n * NCH + k)
                m = len(CHUNKS[k])
                hi, lo = high[k % 2][0:C, :, 0:m * P], rest[k % 2][0:C, :, 0:m * P]
                for o, mats in zip(c_bank, ((0, 2), (1, 0))):
                    terms = [(w, v[:, part, :]) for part, j in enumerate(mats) for w, v in
                             ((w1_high[:, j, :], hi), (w1_high[:, j, :], lo), (w1_rest[:, j, :], hi))]
                    for q, (w, v) in enumerate(terms):
                        last = nc.tensor.matmul(o[0:C, 0:m * P], w, v, start=q == 0, stop=q == len(terms) - 1)
                last.then_inc(c_done, 1)

            def stage_d(n, s, k):
                pe.wait_ge(o_ready, n * NCH + (k + 1))
                for j, k0, m in BANKS_OF[k]:
                    if j >= 2:
                        pe.wait_ge(z_ready, n * NB + (j - 1))
                    else:
                        pe.wait_ge(added, n * GROUPS + 1)
                    o = d_bank[j % 2][:, 0:2 * m * C].rearrange("p (r k c) -> p k r c", r=2, c=C)
                    for i in range(m):
                        nc.tensor.matmul(o[:, i], o_r[k % 2][:, k0 + i, :], w2t[:, 1:3, :], start=True, stop=False)
                        last = nc.tensor.matmul(o[:, i], o_i[k % 2][:, k0 + i, :], w2t[0:C, 0:2, :],
                                                start=False, stop=True)
                    last.then_inc(d_done, 1)

            def merge_real(n):
                pe.wait_ge(turned_real, n + 1)
                o = d_bank[MERGED % 2]
                pe.wait_ge(added, n * GROUPS + 1)
                even, odd = mir[:, 0, :], mir[:, 1, :]
                nc.tensor.matmul(o[:, 0:C], even, real_z[:, 0, 0, :], start=True, stop=False)
                nc.tensor.matmul(o[:, 0:C], odd, real_z[:, 1, 1, :], start=False, stop=True)
                nc.tensor.matmul(o[:, C:2 * C], even, real_z[:, 0, 1, :], start=True, stop=False)
                nc.tensor.matmul(o[:, C:2 * C], odd, real_z[:, 1, 0, :], start=False,
                                 stop=True).then_inc(d_done, 1)

            def spread_scales(n):
                pe.wait_ge(own_ready, n + 1)
                nc.tensor.matmul(slot_scales, pick[:], own[:], start=True, stop=True).then_inc(picked, 1)

            def stage_e(n, g):
                if g == 0:
                    pe.wait_ge(z_split, (n + 1) * NS)
                if g >= E_BANKS:
                    pe.wait_ge(combined_u, n * GROUPS + (g - E_BANKS + 1))
                o = e_bank[g % E_BANKS].rearrange("p (c h) -> p c h", c=GC)
                for slots, cols in ((slice(0, P), slice(0, NCOS)), (slice(HALF, None), slice(NCOS, P))):
                    if g == 0 and cols.start:
                        pe.wait_ge(z_doubled, (n + 1) * (NS - 1))
                    for c in range(GC):
                        hi, lo = (z_parts[:, slots, part, g * GC + c] for part in range(2))
                        nc.tensor.matmul(o[:, c, cols], hi, gh_high[:, cols], start=True, stop=False)
                        nc.tensor.matmul(o[:, c, cols], hi, gh_rest[:, cols], start=False, stop=False)
                        last = nc.tensor.matmul(o[:, c, cols], lo, gh_high[:, cols], start=False, stop=True)
                last.then_inc(e_done, 1)

            def stage_f(n, g):
                pe.wait_ge(u_ready, n * GROUPS + (g + 1))
                if g >= 2:
                    pe.wait_ge(added, n * GROUPS + g)
                q = g % E_BANKS
                hi, lo = high[q % 2][:, q // 2, :], rest[q % 2][:, q // 2, :]
                nc.tensor.matmul(d_bank[g % 2], gw_high[:], hi, start=True, stop=False)
                nc.tensor.matmul(d_bank[g % 2], gw_high[:], lo, start=False, stop=False)
                nc.tensor.matmul(d_bank[g % 2], gw_rest[:], hi, start=False, stop=True).then_inc(f_done, 1)

            pe.wait_ge(consts_in, 16 * CONSTANTS)
            pe.wait_ge(g_ready, 1)
            pe.wait_ge(added, 1)
            with pe.Fori(0, IMAGES * PAIRS) as t:
                for s in range(2):
                    n = t * 2 + s
                    pe.wait_ge(x_loaded[s], (t + 1) * (16 * LOADS))
                    stage_a(n, s)
                    pe.wait_ge(w_ready, n + 2)
                    for k in range(-2, NCH):
                        if k + 2 < NCH:
                            stage_b(n, s, k + 2)
                        if 0 <= k + 1 < NCH:
                            stage_c(n, s, k + 1)
                        if k == 1:
                            merge_real(n)
                        if k >= 0:
                            stage_d(n, s, k)
                    spread_scales(n)
                    for g in range(-E_BANKS, GROUPS):
                        if g >= 0:
                            stage_f(n, g)
                        if g + E_BANKS < GROUPS:
                            stage_e(n, g + E_BANKS)

        @block.scalar
        def _(act):
            def copy_y(n, g):
                act.wait_ge(a_done, n * GROUPS + (g + 1))
                nc.scalar.activation(spec[:, 0:P, g * GC:(g + 1) * GC].rearrange("p k c -> p c k"),
                                     b_bank[g % A_BANKS][:, :].rearrange("p (c k) -> p c k", c=GC),
                                     ACT.Copy).then_inc(y_ready, 1)

            def copy_b(n, k):
                act.wait_ge(b_done, n * NCH + (k + 1))
                m = len(CHUNKS[k])
                sums = psum[0:C, 2 * (k % 2):2 * (k % 2) + 2, 0:m * P].rearrange("c r (k m) -> c r k m", k=m)
                if k:
                    act.wait_ge(x_ready, n * NCH + k)
                    nc.scalar.activation(xs[:, :, 0:m, 0:NCOS], sums[:, :, :, 0:NCOS],
                                         ACT.Copy).then_inc(b_copied, 1)
                else:
                    nc.scalar.activation(xs[:, 0, 0:m, 0:NCOS], sums[:, 0, :, 0:NCOS], ACT.Copy)
                    nc.scalar.activation(xs[:, 0, 0:m, NCOS:P], sums[:, 0, :, 1:HALF], ACT.Copy)
                    nc.scalar.activation(xs[:, 1, 0:m, 1:HALF], sums[:, 0, :, NCOS:P],
                                         ACT.Copy).then_inc(b_copied, 1)

            def split_x(n, k):
                act.wait_ge(combined, n * NCH + (k + 1))
                m = len(CHUNKS[k])
                nc.scalar.activation(high[k % 2][0:C, :, 0:m * P],
                                     xs[:, :, 0:m, :].rearrange("c r k m -> c r (k m)"),
                                     ACT.Copy).then_inc(x_high, 1)

            def relu(n, s, k):
                act.wait_ge(c_done, n * NCH + (k + 1))
                m = len(CHUNKS[k])
                for j, o in enumerate((o_r, o_i)):
                    last = nc.scalar.activation(o[k % 2][0:C, 0:m, :], c_bank[j][0:C, 0:m * P], ACT.Relu,
                                                bias=b1t[:, j:j + 1])
                last.then_inc(o_ready, 1)

            def shrink_above(n, k):
                if k >= 2 and k != NCH - 2:
                    act.wait_ge(z_split, n * NS + (k if k < NCH - 1 else k - 1))
                if k == NCH - 2:
                    act.wait_ge(x_ready, (n + 1) * NCH)
                for j, k0, m in BANKS_OF[k]:
                    act.wait_ge(d_done, n * NB + (j + 1))
                    nc.scalar.activation(z_place(k, k0, m), parts(j, m), ACT.Relu,
                                         bias=low).then_inc(above_ready, 1)

            def split_z(n, i):
                act.wait_ge(scale_ready, n * NS + (i + 1))
                values, _ = unscaled(i)
                nc.scalar.activation(z_slots(i, 0), values.rearrange("p r (k c) -> p r k c", c=C), ACT.Copy,
                                     scale=scale[:, i:i + 1]).then_inc(z_high, 1)

            def copy_e(n, g):
                act.wait_ge(e_done, n * GROUPS + (g + 1))
                q = g % E_BANKS
                if g >= E_BANKS:
                    act.wait_ge(u_ready, n * GROUPS + (g - E_BANKS + 1))
                nc.scalar.activation(us[q][:, :, 0:NCOS],
                                     e_bank[q].rearrange("p (c h) -> p c h", c=GC)[:, :, 0:NCOS], ACT.Copy,
                                     scale=back).then_inc(e_copied, 1)

            def split_u(n, g):
                act.wait_ge(combined_u, n * GROUPS + (g + 1))
                q = g % E_BANKS
                if g >= E_BANKS:
                    act.wait_ge(f_done, n * GROUPS + (g - E_BANKS + 1))
                nc.scalar.activation(high[q % 2][:, q // 2, :], us[q].rearrange("p c h -> p (c h)"),
                                     ACT.Copy).then_inc(u_high, 1)

            act.wait_ge(set_once, 1)
            with act.Fori(0, IMAGES) as b:
                with act.Fori(0, PAIRS) as p:
                    t = b * PAIRS + p
                    for s in range(2):
                        n = t * 2 + s
                        for g in range(GROUPS):
                            copy_y(n, g)
                        act.wait_ge(w2_loaded, (n + 1) * (16 * W2_DMAS))
                        for k in range(-2, NCH):
                            if k + 2 < NCH:
                                copy_b(n, k + 2)
                            elif k + 1 < NCH:
                                relu(n, s, k + 1)
                            if k == 2:
                                split_z(n, 0)
                            if 2 <= k < LATE:
                                split_z(n, k - 1)
                            if k + 2 < NCH:
                                split_x(n, k + 2)
                                if k + 1 >= 0:
                                    relu(n, s, k + 1)
                            if k >= 0:
                                shrink_above(n, k)
                            if k >= LATE:
                                split_z(n, k - 1)
                        split_z(n, NS - 1)
                        act.wait_ge(back_ready, n + 1)
                        for g in range(GROUPS + 1):
                            if g < GROUPS:
                                copy_e(n, g)
                            if g:
                                split_u(n, g - 1)
                        act.wait_ge(added, (n + 1) * GROUPS + 1)
                        for q in range(LOADS):
                            act.dma_start(out_v[b, p, s, :, q * HL:(q + 1) * HL, :],
                                          tile[s][:, q * HL:(q + 1) * HL, :]).then_inc(x_stored[s], 16)
            for s in range(2):
                act.wait_ge(x_stored[s], 16 * LOADS * IMAGES * PAIRS + 1)

        @block.vector
        def _(dve):
            def split_w(n):
                dve.wait_ge(w1_loaded, (n + 1) * 16)
                nc.vector.tensor_copy(w1_high[:, 0:2, :], w1t[:])
                nc.vector.tensor_scalar(w1_high[:, 2, :], w1t[:, 1, :], -1.0, None, ALU.mult).then_inc(w_high, 1)
                dve.wait_ge(w_high, n + 1)
                nc.vector.tensor_tensor(w1_rest[:, 0:2, :], w1t[:], w1_high[:, 0:2, :].bitcast(F32), ALU.subtract)
                nc.vector.scalar_tensor_tensor(w1_rest[:, 2, :], w1t[:, 1, :], -1.0,
                                               w1_high[:, 2, :].bitcast(F32), ALU.mult, ALU.subtract)
                dve.wait_ge(w2_loaded, (n + 1) * (16 * W2_DMAS))
                nc.vector.tensor_scalar(w2t[0:C, 0, :], w2t[0:C, 2, :], -1.0, None, ALU.mult).then_inc(w_ready, 1)

            def sums_of(k, part):
                m = len(CHUNKS[k])
                other = b_bank[2 * (k % 2) + (1 - part if k else 0)][0:C, 0:m * P]
                return xs[:, part, 0:m, :], other.rearrange("c (k m) -> c k m", k=m)[:, :, NCOS:P]

            def combine_negative(n, k):
                dve.wait_ge(b_copied, n * NCH + (k + 1))
                (r, from_im), (i, from_re) = sums_of(k, 0), sums_of(k, 1)
                if k == 0:
                    nc.vector.memset(i[:, :, 0:NCOS:HALF], 0.0)
                    nc.vector.tensor_scalar(i[:, :, NCOS:P], from_re, -1.0, None, ALU.mult).then_inc(combined, 1)
                    return
                nc.vector.tensor_tensor(r[:, :, NCOS:P], r[:, :, 1:HALF], from_im, ALU.add)
                nc.vector.tensor_tensor(i[:, :, NCOS:P], i[:, :, 1:HALF], from_re, ALU.subtract)

            def combine_positive_real(n, k):
                r, from_im = sums_of(k, 0)
                nc.vector.tensor_tensor(r[:, :, 1:HALF], r[:, :, 1:HALF], from_im, ALU.subtract)

            def combine_positive_imag(n, k):
                i, from_re = sums_of(k, 1)
                nc.vector.tensor_tensor(i[:, :, 1:HALF], i[:, :, 1:HALF], from_re, ALU.add).then_inc(combined, 1)

            def rest_x(n, k):
                dve.wait_ge(x_high, n * NCH + (k + 1))
                m = len(CHUNKS[k])
                nc.vector.tensor_tensor(rest[k % 2][0:C, :, 0:m * P],
                                        xs[:, :, 0:m, :].rearrange("c r k m -> c r (k m)"),
                                        high[k % 2][0:C, :, 0:m * P].bitcast(F32),
                                        ALU.subtract).then_inc(x_ready, 1)

            def shrink(n, k):
                if k == NCH - 2:
                    nc.vector.memset(late_zs[:, 0:1], LEAST)
                for j, k0, m in BANKS_OF[k]:
                    dve.wait_ge(above_ready, n * (NB - 1) + (j + 1 if j == 0 else j))
                    dst = z_place(k, k0, m)
                    nc.vector.scalar_tensor_tensor(dst, parts(j, m), LAMBDA, dst, ALU.add,
                                                   ALU.min).then_inc(z_ready, 1)

            def turn_real(n):
                dve.wait_ge(z_ready, n * NB + 1)
                nc.vector.tensor_scalar(real_z[:, 1, 1, :], real_z[:, 1, 1, :], -1.0, None,
                                        ALU.mult).then_inc(turned_real, 1)

            def copy_merged(n):
                dve.wait_ge(d_done, n * NB + (MERGED + 1))
                values, _ = unscaled(0)
                nc.vector.tensor_copy(values, parts(MERGED, 1)).then_inc(z_ready, 1)

            def find_largest(n, i):
                dve.wait_ge(z_ready, n * NB + (BANKS_OF[i][-1][0] + 1 if i else MERGED + 1))
                _, row = unscaled(i)
                nc.vector.tensor_reduce(largest[:, i:i + 1], row, AX.X, ALU.max,
                                        apply_absolute_value=True).then_inc(largest_ready, 1)

            def find_power(n, i):
                dve.wait_ge(top_ready, n * NS + (i + 1))
                nc.vector.tensor_scalar(power[:, i:i + 1].bitcast(I32), top[:, i:i + 1].bitcast(I32),
                                        EXPONENT_MASK, None, ALU.bitwise_and).then_inc(power_ready, 1)

            def find_scale(n, i):
                dve.wait_ge(power_ready, n * NS + (i + 1))
                nc.vector.tensor_scalar(scale[:, i:i + 1].bitcast(I32), power[:, i:i + 1].bitcast(I32),
                                        -1, SCALE_BITS, ALU.mult, ALU.add).then_inc(scale_ready, 1)

            def rest_z(n, i):
                dve.wait_ge(z_high, n * NS + (i + 1))
                values, _ = unscaled(i)
                hi, lo = z_slots(i, 0), z_slots(i, 1)
                for part in range(2):
                    last = nc.vector.scalar_tensor_tensor(
                        lo[:, part], values[:, part, :].rearrange("p (k c) -> p k c", c=C), scale[:, i:i + 1],
                        hi[:, part], ALU.mult, ALU.subtract)
                last.then_inc(z_split, 1)

            def double_z(n, i, last):
                dve.wait_ge(z_split, n * NS + (last + 1))
                ky, end = CHUNKS[i][0], (CHUNKS[last][-1] if last else 0) + 1
                nc.vector.tensor_copy(z_parts[:, P + ky:P + end, :, :],
                                      z_parts[:, ky:end, :, :]).then_inc(z_doubled, 1)

            def scales_by_slot(n):
                nc.vector.tensor_tensor(own[:], power[0:NS, :], diag[:], ALU.mult).then_inc(own_ready, 1)

            def take_scales(n):
                dve.wait_ge(picked, n + 1)
                nc.vector.tensor_reduce(back, slot_scales, AX.X, ALU.add).then_inc(back_ready, 1)
                dve.wait_ge(back_ready, n + 1)
                nc.vector.tensor_scalar(turned, sgn, back, None, ALU.mult).then_inc(turned_ready, 1)
                dve.wait_ge(turned_ready, n + 2)

            def combine_u(n, g):
                dve.wait_ge(e_copied, n * GROUPS + (g + 1))
                o = us[g % E_BANKS]
                sin = e_bank[g % E_BANKS].rearrange("p (c h) -> p c h", c=GC)[:, :, NCOS:P]
                nc.vector.scalar_tensor_tensor(o[:, :, P - 1:HALF:-1], sin, turned[:, 1:2], o[:, :, 1:HALF],
                                               ALU.mult, ALU.add)
                nc.vector.scalar_tensor_tensor(o[:, :, 1:HALF], sin, turned[:, 0:1], o[:, :, 1:HALF],
                                               ALU.mult, ALU.add).then_inc(combined_u, 1)

            def add_x(n, s, g):
                dve.wait_ge(f_done, n * GROUPS + (g + 1))
                dst = tile[s][:, :, g * GC:(g + 1) * GC].rearrange("p h c -> p c h")
                nc.vector.tensor_tensor(dst, dst, d_bank[g % 2].rearrange("p (c h) -> p c h", c=GC),
                                        ALU.add).then_inc(added, 1)

            for i in range(2):
                nc.vector.memset(o_r[i][C:C + 1, :, :], 1.0).then_inc(x_stored[i], 1)
            nc.vector.memset(started[:, 0:1], 0.0).then_inc(added, 1)
            nc.vector.memset(started[:, 1:2], 0.0).then_inc(w_ready, 1)
            dve.wait_ge(consts_in, 16 * CONSTANTS)
            nc.vector.tensor_copy(pick[:], picks)
            nc.vector.tensor_copy(gw_high[:], gw).then_inc(g_high, 1)
            dve.wait_ge(g_high, 1)
            nc.vector.tensor_tensor(gw_rest[:], gw, gw_high[:].bitcast(F32), ALU.subtract).then_inc(g_ready, 1)
            dve.wait_ge(g_ready, 1)
            nc.vector.memset(turned, 0.0).then_inc(turned_ready, 1)
            with dve.Fori(0, IMAGES * PAIRS) as t:
                for s in range(2):
                    n = t * 2 + s
                    split_w(n)
                    for k in range(-2, NCH):
                        if k + 2 < NCH:
                            combine_negative(n, k + 2)
                        if k == 2:
                            find_power(n, 0)
                        if 2 <= k < NCH - 1:
                            find_power(n, k - 1)
                        if 0 < k + 2 < NCH:
                            combine_positive_real(n, k + 2)
                        if k == 2:
                            find_scale(n, 0)
                        if 2 <= k < NCH - 1:
                            find_scale(n, k - 1)
                        if 0 < k + 2 < NCH:
                            combine_positive_imag(n, k + 2)
                        if k == 2:
                            rest_z(n, 0)
                        if 2 <= k < LATE:
                            rest_z(n, k - 1)
                        if k + 2 < NCH:
                            rest_x(n, k + 2)
                        if k == 2:
                            double_z(n, 0, 0)
                        if 3 <= k:
                            double_z(n, k - 2, k - 2)
                        if k == 1:
                            copy_merged(n)
                            find_largest(n, 0)
                        if k >= 0:
                            shrink(n, k)
                        if k == 0:
                            turn_real(n)
                        if k == LATE:
                            rest_z(n, k - 1)
                        if k >= 1:
                            find_largest(n, k)
                    for i in (NS - 2, NS - 1):
                        find_power(n, i)
                        find_scale(n, i)
                    scales_by_slot(n)
                    rest_z(n, NS - 2)
                    rest_z(n, NS - 1)
                    double_z(n, NS - 2, NS - 1)
                    take_scales(n)
                    for g in range(GROUPS + E_BANKS - 1):
                        if g < GROUPS:
                            combine_u(n, g)
                        if g >= E_BANKS - 1:
                            add_x(n, s, g - E_BANKS + 1)


_INS = ["x", "L0_conv_w1", "L0_conv_b1", "L0_conv_w2", "L0_conv_b2"]


def _tables(p):
    import numpy as np
    half = p // 2
    angle = 2 * np.pi * (np.outer(np.arange(p), np.arange(half + 1)) % p) / p
    cos, sin = np.cos(angle), np.sin(angle)
    kx = np.concatenate([np.arange(half + 1), -np.arange(1, half)])
    f_x = np.concatenate([cos[:, :half + 1], -sin[:, 1:half]], 1)
    back = 2 * np.pi * (np.outer(kx, np.arange(half + 1)) % p) / p
    g_h = np.concatenate([np.cos(back), np.sin(back)[:, 1:half]], 1)
    g_h_high = g_h.astype(np.float16)
    g_h_rest = (g_h - g_h_high).astype(np.float16)
    g_w = 2 * f_x.T / p ** 2
    g_w[0] /= 2
    g_w[half] /= 2
    partner = np.array([list(kx % p).index((-k) % p) for k in kx])
    same, swap = np.eye(p), np.eye(p)[partner]
    even, odd = (same + swap) / 2, (same - swap) / 2
    mirror = np.stack([even, odd.T], 1)
    turn = np.ones((p, 2))
    turn[:half, 0] = -1
    turn[half:, 1] = -1
    group = np.array([(k % half + 3) // 4 for k in range(p)])
    chunk_of_slot = (group[None, :] == np.arange(half // 4 + 1)[:, None])
    diagonal = np.eye(half // 4 + 1) * 2.0 ** -14
    out = {k: np.ascontiguousarray(v, np.float32) for k, v in
           dict(f_x=f_x, g_h_high=g_h_high, g_h_rest=g_h_rest, g_w=g_w, mirror=mirror, turn=turn,
                chunk_of_slot=chunk_of_slot, diagonal=diagonal).items()}
    out["g_h_high"], out["g_h_rest"] = g_h_high, g_h_rest
    return out


def kernel(**inputs):
    import numpy as _np
    import concourse.bacc as _bacc
    from concourse import mybir as _mybir
    from concourse.bass_utils import run_bass_kernel_spmd as _run

    nc = _bacc.Bacc("TRN2", target_bir_lowering=False, num_devices=1)
    arrays, args = {}, []
    for name in _INS:
        arrays[f"in_{name}_dram"] = _np.ascontiguousarray(inputs[name])
    for name, a in _tables(128).items():
        arrays[f"const_{name}_dram"] = a
    for name, a in arrays.items():
        args.append(nc.dram_tensor(name, a.shape, _mybir.dt.from_np(a.dtype), kind="ExternalInput").ap())
    shape = inputs["x"].shape
    args.append(nc.dram_tensor("out_0_dram", shape, _mybir.dt.float32, kind="ExternalOutput").ap())
    fourier_mixer_kernel(nc, *args)
    r = _run(nc, [arrays], core_ids=[0])
    return r.results[0]["out_0_dram"]
```

```python
import concourse.bass as bass
from concourse import mybir
from contextlib import ExitStack


def fourier_mixer_kernel(nc, x, w1, b1, w2, b2, f_x, g_h_high, g_h_rest, g_w, mirror, turn,
                         chunk_of_slot, diagonal, out):
    F32, F32R, F16, BF16 = mybir.dt.float32, mybir.dt.float32r, mybir.dt.float16, mybir.dt.bfloat16
    I32 = mybir.dt.int32
    ALU = mybir.AluOpType
    ACT = mybir.ActivationFunctionType
    AX = mybir.AxisListType

    IMAGES, H, W, CHANNELS = x.shape
    HEADS, C = w1.shape[1], w1.shape[2]
    P = 128
    assert H == W == P
    HALF = P // 2
    LAMBDA = 0.01
    LEAST = 1e-30
    NCOS, NSIN = HALF + 1, HALF - 1

    GC = 4
    GROUPS = C // GC
    A_BANKS = 4
    CK = 4
    CHUNKS = [[0, HALF]] + [list(range(k, min(k + CK, HALF))) for k in range(1, HALF, CK)]
    NCH = len(CHUNKS)
    DK = 2
    MERGED = 1
    BANKS_OF = [[(0, 0, DK)]]
    for ks in CHUNKS[1:]:
        BANKS_OF.append([(1 + sum(map(len, BANKS_OF)) + i, k, min(DK, len(ks) - k))
                         for i, k in enumerate(range(0, len(ks), DK))])
    NB = 1 + sum(map(len, BANKS_OF))
    assert NB % 2 == 0
    NS = NCH
    TAIL = NCH - 3
    assert TAIL % 2 == 0
    SHARED_EXPONENT = 14
    EXPONENT_MASK = 0x7F800000
    SCALE_BITS = (2 * 127 + SHARED_EXPONENT) << 23
    E_BANKS = A_BANKS
    LOADS = 4
    HL = H // LOADS
    PAIRS = HEADS // 2

    with ExitStack() as ctx:
        def sb(name, shape, dt=F32):
            return ctx.enter_context(nc.sbuf_tensor(name, shape, dt))

        def sem(name):
            return ctx.enter_context(nc.semaphore(name))

        tile = [sb(f"tile{s}", [P, H, C]) for s in range(2)]
        spec = sb("spec", [P, P + HALF, C])
        zs = sb("zs", [P, 1 + 2 * CK * C])
        real_zs = sb("real_zs", [P, 1 + 2 * 2 * C])
        real_z = real_zs[:, 1:].rearrange("p (r k c) -> p r k c", r=2, c=C)
        room = sb("room", [P, 4 * CK * P])
        xs_u = room[:, 0:2 * CK * P].rearrange("p (r k) -> p r k", r=2)
        xs = xs_u[0:C, :, :].rearrange("c r (k m) -> c r k m", m=P)
        high = [sb(f"high{i}", [P, 2, CK * P], F32R) for i in range(2)]
        rest = [sb(f"rest{i}", [P, 2, CK * P], F32R) for i in range(2)]
        last_zs = [room[:, 0:zs.shape[1]], zs, room[:, zs.shape[1]:3 * CK * P]]
        o_r = [sb(f"o_r{i}", [C + 1, CK, P]) for i in range(2)]
        o_u = [room[:, i * CK * P:(i + 1) * CK * P] for i in (3, 2)]
        o_i = [o[0:C, :].rearrange("c (k m) -> c k m", m=P) for o in o_u]
        us = [o_u[0], o_u[1], xs_u[:, 0, :], xs_u[:, 1, :]]
        us = [v.rearrange("p (c h) -> p c h", c=GC) for v in us]
        w1t = real_zs[0:C, 1:1 + 2 * C].rearrange("c (r o) -> c r o", r=2)
        w1_high = sb("w1_high", [C, 3, C], F32R)
        w1_rest = sb("w1_rest", [C, 3, C], F32R)
        w2t = sb("w2t", [C + 1, 3, C])
        b1t = sb("b1t", [C, 2])
        fx = sb("fx", [P, P])
        gh_high = sb("gh_high", [P, P], F16)
        gh_rest = sb("gh_rest", [P, P], F16)
        gw = real_zs[:, 1:1 + P]
        gw_high = sb("gw_high", [P, P], F32R)
        gw_rest = sb("gw_rest", [P, P], F32R)
        mir = sb("mir", [P, 2, P])
        single = sb("single", [P, 10])
        low = single[:, 0:1]
        one = single[:, 1:2]
        started = single[:, 3:5]
        back = single[:, 5:6]
        sgn = single[:, 6:8]
        turned = single[:, 8:10]
        scales = sb("scales", [P, 4, NS])
        largest = scales[:, 0, :]
        top = scales[:, 1, :]
        power = scales[:, 2, :]
        scale = scales[:, 3, :]
        own = sb("own", [NS, NS], BF16)
        pick = sb("pick", [NS, P], BF16)
        picks = real_zs[0:NS, 1 + P:1 + 2 * P]
        diag = sb("diag", [NS, NS])

        psum = ctx.enter_context(nc.psum_tensor("banks", [P, 8, 512], F32))
        b_bank = [psum[:, i, :] for i in range(4)]
        c_bank = [psum[:, 4 + i, :] for i in range(2)]
        d_bank = [psum[:, 6 + i, :] for i in range(2)]
        e_bank = b_bank
        slot_scales = c_bank[0][:, 0:NS]

        consts_in = sem("consts_in")
        set_once = sem("set_once")
        x_loaded = [sem(f"x_loaded{s}") for s in range(2)]
        x_stored = [sem(f"x_stored{s}") for s in range(2)]
        w1_loaded = sem("w1_loaded")
        w2_loaded = sem("w2_loaded")
        w_high = sem("w_high")
        w_ready = sem("w_ready")
        g_high = sem("g_high")
        g_ready = sem("g_ready")
        a_done = sem("a_done")
        y_ready = sem("y_ready")
        b_done = sem("b_done")
        b_copied = sem("b_copied")
        combined = sem("combined")
        x_high = sem("x_high")
        x_ready = sem("x_ready")
        c_done = sem("c_done")
        o_ready = sem("o_ready")
        d_done = sem("d_done")
        above_ready = sem("above_ready")
        z_ready = sem("z_ready")
        turned_real = sem("turned_real")
        largest_ready = sem("largest_ready")
        top_ready = sem("top_ready")
        power_ready = sem("power_ready")
        scale_ready = sem("scale_ready")
        z_high = sem("z_high")
        z_split = sem("z_split")
        z_doubled = sem("z_doubled")
        own_ready = sem("own_ready")
        picked = sem("picked")
        back_ready = sem("back_ready")
        turned_ready = sem("turned_ready")
        e_done = sem("e_done")
        e_copied = sem("e_copied")
        combined_u = sem("combined_u")
        u_high = sem("u_high")
        u_ready = sem("u_ready")
        f_done = sem("f_done")
        added = sem("added")

        x_v = x.rearrange("b h w (g s c) -> b g s w h c", s=2, c=C)
        out_v = out.rearrange("b h w (g s c) -> b g s w h c", s=2, c=C)
        w1_v = w1.rearrange("r (g s) i o -> g s i r o", s=2)
        b1_v = b1.rearrange("r (g s) o -> g s o r", s=2)
        w2_v = w2.rearrange("r (g s) i o -> g s r i o", s=2)
        b2_v = b2.rearrange("r (g s) (a o) -> g s a r o", s=2, a=1)
        W2_DMAS = 4
        CONSTANTS = 8

        def parts(j, m):
            return d_bank[j % 2][:, 0:2 * m * C].rearrange("p (r c) -> p r c", r=2)

        def z_place(k, k0, m):
            if k == 0:
                return real_z.rearrange("p r k c -> p r (k c)")
            return unscaled(k)[0][:, :, k0 * C:(k0 + m) * C]

        def unscaled(i):
            m = len(CHUNKS[i]) if i else 1
            row = (last_zs[i - TAIL] if i >= TAIL else zs if i else real_zs)[:, 0:1 + 2 * m * C]
            return row[:, 1:].rearrange("p (r c) -> p r c", r=2), row

        z_parts = spec[:, :, :].bitcast(F16).rearrange("p k (q c) -> p k q c", q=2)

        def z_slots(i, part):
            ky, m = (CHUNKS[i][0], len(CHUNKS[i])) if i else (0, 1)
            return z_parts[:, 0:P, part, :].rearrange("p (r k) c -> p r k c", r=2)[:, :, ky:ky + m, :]

        block = ctx.enter_context(nc.Block())

        @block.sync
        def _(sp):
            for dst, src in ((fx[:], f_x), (gh_high[:], g_h_high), (gh_rest[:], g_h_rest),
                             (gw, g_w), (mir[:], mirror), (sgn, turn), (picks, chunk_of_slot),
                             (diag[:], diagonal)):
                sp.dma_start(dst, src).then_inc(consts_in, 16)
            with sp.Fori(0, IMAGES) as b:
                with sp.Fori(0, PAIRS) as g:
                    t = b * PAIRS + g
                    for s in range(2):
                        n = t * 2 + s
                        sp.wait_ge(x_stored[s], t * (16 * LOADS) + 1)
                        for q in range(LOADS):
                            sp.dma_start(tile[s][:, q * HL:(q + 1) * HL, :],
                                         x_v[b, g, s, :, q * HL:(q + 1) * HL, :]).then_inc(x_loaded[s], 16)
                        sp.wait_ge(turned_ready, n + 1)
                        sp.dma_start(w1t, w1_v[g, s]).then_inc(w1_loaded, 16)
                        sp.dma_start(b1t[:], b1_v[g, s], allow_slow_non_contiguous=True).then_inc(w2_loaded, 16)
                        for r in range(2):
                            sp.dma_start(w2t[0:C, 1 + r, :], w2_v[g, s, r]).then_inc(w2_loaded, 16)
                        sp.dma_start(w2t[C:C + 1, 1:3, :], b2_v[g, s]).then_inc(w2_loaded, 16)

        @block.gpsimd
        def _(pool):
            nc.gpsimd.memset(low, -LAMBDA)
            nc.gpsimd.memset(one, 1.0)
            nc.gpsimd.memset(zs[:, 0:1], LEAST)
            nc.gpsimd.memset(real_zs[:, 0:1], LEAST).then_inc(set_once, 1)
            pool.wait_ge(set_once, 1)

            def find_top(n, i):
                pool.wait_ge(largest_ready, n * NS + (i + 1))
                nc.gpsimd.tensor_tensor(scale[:, i:i + 1], one, one, ALU.mult)
                nc.gpsimd.partition_all_reduce(top[:, i:i + 1], largest[:, i:i + 1], P,
                                               bass.bass_isa.ReduceOp.max).then_inc(top_ready, 1)

            def rest_u(n, g):
                q = g % E_BANKS
                pool.wait_ge(u_high, n * GROUPS + (g + 1))
                nc.gpsimd.tensor_tensor(rest[q % 2][:, q // 2, :], us[q].rearrange("p c h -> p (c h)"),
                                        high[q % 2][:, q // 2, :].bitcast(F32),
                                        ALU.subtract).then_inc(u_ready, 1)

            with pool.Fori(0, IMAGES * PAIRS) as t:
                for s in range(2):
                    n = t * 2 + s
                    for i in range(NS):
                        find_top(n, i)
                    for g in range(GROUPS):
                        rest_u(n, g)

        @block.tensor
        def _(pe):
            def stage_a(n, s, g):
                if g >= A_BANKS:
                    pe.wait_ge(y_ready, n * GROUPS + (g - A_BANKS + 1))
                for c in range(GC):
                    last = nc.tensor.matmul(b_bank[g % A_BANKS][:, c * P:(c + 1) * P],
                                            tile[s][:, :, g * GC + c], fx[:], start=True, stop=True)
                last.then_inc(a_done, 1)

            def stage_b(n, k):
                if k == 0:
                    pe.wait_ge(y_ready, (n + 1) * GROUPS)
                if k >= 2:
                    pe.wait_ge(combined, n * NCH + (k - 1))
                re, im = b_bank[2 * (k % 2)], b_bank[2 * (k % 2) + 1]
                for i, ky in enumerate(CHUNKS[k]):
                    last = nc.tensor.matmul(re[0:C, i * P:(i + 1) * P], spec[:, ky, :], fx[:],
                                            start=True, stop=True)
                    if k:
                        last = nc.tensor.matmul(im[0:C, i * P:(i + 1) * P], spec[:, HALF + ky, :], fx[:],
                                                start=True, stop=True)
                last.then_inc(b_done, 1)

            def stage_c(n, k):
                pe.wait_ge(x_ready, n * NCH + (k + 1))
                if k:
                    pe.wait_ge(o_ready, n * NCH + k)
                m = len(CHUNKS[k])
                hi, lo = high[k % 2][0:C, :, 0:m * P], rest[k % 2][0:C, :, 0:m * P]
                for o, mats in zip(c_bank, ((0, 2), (1, 0))):
                    terms = [(w, v[:, part, :]) for part, j in enumerate(mats) for w, v in
                             ((w1_high[:, j, :], hi), (w1_high[:, j, :], lo), (w1_rest[:, j, :], hi))]
                    for q, (w, v) in enumerate(terms):
                        last = nc.tensor.matmul(o[0:C, 0:m * P], w, v, start=q == 0, stop=q == len(terms) - 1)
                last.then_inc(c_done, 1)

            def stage_d(n, k):
                pe.wait_ge(o_ready, n * NCH + (k + 1))
                for j, k0, m in BANKS_OF[k]:
                    if j >= 2:
                        pe.wait_ge(z_ready, n * NB + (j - 1))
                    else:
                        pe.wait_ge(added, n * GROUPS + 1)
                    o = d_bank[j % 2][:, 0:2 * m * C].rearrange("p (r k c) -> p k r c", r=2, c=C)
                    for i in range(m):
                        nc.tensor.matmul(o[:, i], o_r[k % 2][:, k0 + i, :], w2t[:, 1:3, :], start=True, stop=False)
                        last = nc.tensor.matmul(o[:, i], o_i[k % 2][:, k0 + i, :], w2t[0:C, 0:2, :],
                                                start=False, stop=True)
                    last.then_inc(d_done, 1)

            def merge_real(n):
                pe.wait_ge(turned_real, n + 1)
                o = d_bank[MERGED % 2]
                pe.wait_ge(added, n * GROUPS + 1)
                even, odd = mir[:, 0, :], mir[:, 1, :]
                nc.tensor.matmul(o[:, 0:C], even, real_z[:, 0, 0, :], start=True, stop=False)
                nc.tensor.matmul(o[:, 0:C], odd, real_z[:, 1, 1, :], start=False, stop=True)
                nc.tensor.matmul(o[:, C:2 * C], even, real_z[:, 0, 1, :], start=True, stop=False)
                nc.tensor.matmul(o[:, C:2 * C], odd, real_z[:, 1, 0, :], start=False,
                                 stop=True).then_inc(d_done, 1)

            def spread_scales(n):
                pe.wait_ge(own_ready, n + 1)
                nc.tensor.matmul(slot_scales, pick[:], own[:], start=True, stop=True).then_inc(picked, 1)

            def stage_e(n, g):
                if g == 0:
                    pe.wait_ge(z_split, (n + 1) * NS)
                if g >= E_BANKS:
                    pe.wait_ge(combined_u, n * GROUPS + (g - E_BANKS + 1))
                o = e_bank[g % E_BANKS].rearrange("p (c h) -> p c h", c=GC)
                for slots, cols in ((slice(0, P), slice(0, NCOS)), (slice(HALF, None), slice(NCOS, P))):
                    if g == 0 and cols.start:
                        pe.wait_ge(z_doubled, (n + 1) * (NS - 1))
                    for c in range(GC):
                        hi, lo = (z_parts[:, slots, part, g * GC + c] for part in range(2))
                        nc.tensor.matmul(o[:, c, cols], hi, gh_high[:, cols], start=True, stop=False)
                        nc.tensor.matmul(o[:, c, cols], hi, gh_rest[:, cols], start=False, stop=False)
                        last = nc.tensor.matmul(o[:, c, cols], lo, gh_high[:, cols], start=False, stop=True)
                last.then_inc(e_done, 1)

            def stage_f(n, g):
                pe.wait_ge(u_ready, n * GROUPS + (g + 1))
                if g >= 2:
                    pe.wait_ge(added, n * GROUPS + g)
                q = g % E_BANKS
                hi, lo = high[q % 2][:, q // 2, :], rest[q % 2][:, q // 2, :]
                nc.tensor.matmul(d_bank[g % 2], gw_high[:], hi, start=True, stop=False)
                nc.tensor.matmul(d_bank[g % 2], gw_high[:], lo, start=False, stop=False)
                nc.tensor.matmul(d_bank[g % 2], gw_rest[:], hi, start=False, stop=True).then_inc(f_done, 1)

            pe.wait_ge(consts_in, 16 * CONSTANTS)
            pe.wait_ge(g_ready, 1)
            pe.wait_ge(added, 1)
            with pe.Fori(0, IMAGES * PAIRS) as t:
                for s in range(2):
                    n = t * 2 + s
                    if s == 0:
                        pe.wait_ge(x_loaded[0], (t + 1) * (16 * LOADS))
                    for g in range(A_BANKS if s else 0, GROUPS):
                        stage_a(n, s, g)
                    pe.wait_ge(w_ready, n + 2)
                    for k in range(-3, NCH):
                        if k + 3 < NCH:
                            stage_b(n, k + 3)
                        if 0 <= k + 1 < NCH:
                            stage_c(n, k + 1)
                        if k == 1:
                            merge_real(n)
                        if k >= 0:
                            stage_d(n, k)
                    spread_scales(n)
                    for g in range(-E_BANKS, GROUPS):
                        if g >= 0:
                            stage_f(n, g)
                        if g + E_BANKS < GROUPS:
                            stage_e(n, g + E_BANKS)
                        elif s == 0:
                            if g + E_BANKS == GROUPS:
                                pe.wait_ge(x_loaded[1], (t + 1) * (16 * LOADS))
                            stage_a(n + 1, 1, g + E_BANKS - GROUPS)

        @block.scalar
        def _(act):
            def copy_y(n, g):
                act.wait_ge(a_done, n * GROUPS + (g + 1))
                nc.scalar.activation(spec[:, 0:P, g * GC:(g + 1) * GC].rearrange("p k c -> p c k"),
                                     b_bank[g % A_BANKS][:, :].rearrange("p (c k) -> p c k", c=GC),
                                     ACT.Copy).then_inc(y_ready, 1)

            def copy_b(n, k):
                act.wait_ge(b_done, n * NCH + (k + 1))
                m = len(CHUNKS[k])
                sums = psum[0:C, 2 * (k % 2):2 * (k % 2) + 2, 0:m * P].rearrange("c r (k m) -> c r k m", k=m)
                if k:
                    act.wait_ge(x_ready, n * NCH + k)
                    nc.scalar.activation(xs[:, :, 0:m, 0:NCOS], sums[:, :, :, 0:NCOS],
                                         ACT.Copy).then_inc(b_copied, 1)
                else:
                    nc.scalar.activation(xs[:, 0, 0:m, 0:NCOS], sums[:, 0, :, 0:NCOS], ACT.Copy)
                    nc.scalar.activation(xs[:, 0, 0:m, NCOS:P], sums[:, 0, :, 1:HALF], ACT.Copy)
                    nc.scalar.activation(xs[:, 1, 0:m, 1:HALF], sums[:, 0, :, NCOS:P],
                                         ACT.Copy).then_inc(b_copied, 1)

            def split_x(n, k):
                act.wait_ge(combined, n * NCH + (k + 1))
                m = len(CHUNKS[k])
                nc.scalar.activation(high[k % 2][0:C, :, 0:m * P],
                                     xs[:, :, 0:m, :].rearrange("c r k m -> c r (k m)"),
                                     ACT.Copy).then_inc(x_high, 1)

            def relu(n, k):
                act.wait_ge(c_done, n * NCH + (k + 1))
                m = len(CHUNKS[k])
                for j, o in enumerate((o_r, o_i)):
                    last = nc.scalar.activation(o[k % 2][0:C, 0:m, :], c_bank[j][0:C, 0:m * P], ACT.Relu,
                                                bias=b1t[:, j:j + 1])
                last.then_inc(o_ready, 1)

            def shrink_above(n, k):
                if 2 <= k < TAIL:
                    act.wait_ge(z_split, n * NS + k)
                if k == TAIL:
                    act.wait_ge(x_ready, (n + 1) * NCH)
                if k == TAIL + 1:
                    act.wait_ge(z_split, n * NS + TAIL)
                for j, k0, m in BANKS_OF[k]:
                    act.wait_ge(d_done, n * NB + (j + 1))
                    nc.scalar.activation(z_place(k, k0, m), parts(j, m), ACT.Relu,
                                         bias=low).then_inc(above_ready, 1)

            def split_z(n, i):
                act.wait_ge(scale_ready, n * NS + (i + 1))
                values, _ = unscaled(i)
                nc.scalar.activation(z_slots(i, 0), values.rearrange("p r (k c) -> p r k c", c=C), ACT.Copy,
                                     scale=scale[:, i:i + 1]).then_inc(z_high, 1)

            def copy_e(n, g):
                act.wait_ge(e_done, n * GROUPS + (g + 1))
                q = g % E_BANKS
                if g >= E_BANKS:
                    act.wait_ge(u_ready, n * GROUPS + (g - E_BANKS + 1))
                nc.scalar.activation(us[q][:, :, 0:NCOS],
                                     e_bank[q].rearrange("p (c h) -> p c h", c=GC)[:, :, 0:NCOS], ACT.Copy,
                                     scale=back).then_inc(e_copied, 1)

            def split_u(n, g):
                act.wait_ge(combined_u, n * GROUPS + (g + 1))
                q = g % E_BANKS
                if g >= E_BANKS:
                    act.wait_ge(f_done, n * GROUPS + (g - E_BANKS + 1))
                nc.scalar.activation(high[q % 2][:, q // 2, :], us[q].rearrange("p c h -> p (c h)"),
                                     ACT.Copy).then_inc(u_high, 1)

            act.wait_ge(set_once, 1)
            with act.Fori(0, IMAGES) as b:
                with act.Fori(0, PAIRS) as p:
                    t = b * PAIRS + p
                    for s in range(2):
                        n = t * 2 + s
                        for g in range(A_BANKS if s else 0, GROUPS):
                            copy_y(n, g)
                        act.wait_ge(w2_loaded, (n + 1) * (16 * W2_DMAS))
                        for k in range(-2, TAIL):
                            copy_b(n, k + 2)
                            if k == 2:
                                split_z(n, 0)
                            if k >= 2:
                                split_z(n, k - 1)
                            split_x(n, k + 2)
                            if k + 1 >= 0:
                                relu(n, k + 1)
                            if k >= 0:
                                shrink_above(n, k)
                        copy_b(n, TAIL + 2)
                        split_x(n, TAIL + 2)
                        relu(n, TAIL + 1)
                        shrink_above(n, TAIL)
                        split_z(n, TAIL - 1)
                        relu(n, TAIL + 2)
                        shrink_above(n, TAIL + 1)
                        split_z(n, TAIL)
                        shrink_above(n, TAIL + 2)
                        split_z(n, TAIL + 1)
                        split_z(n, TAIL + 2)
                        act.wait_ge(back_ready, n + 1)
                        for g in range(GROUPS + 1):
                            if g < GROUPS:
                                copy_e(n, g)
                            if g:
                                split_u(n, g - 1)
                        if s == 0:
                            for g in range(A_BANKS):
                                copy_y(n + 1, g)
                        act.wait_ge(added, (n + 1) * GROUPS + 1)
                        for q in range(LOADS):
                            act.dma_start(out_v[b, p, s, :, q * HL:(q + 1) * HL, :],
                                          tile[s][:, q * HL:(q + 1) * HL, :]).then_inc(x_stored[s], 16)
            for s in range(2):
                act.wait_ge(x_stored[s], 16 * LOADS * IMAGES * PAIRS + 1)

        @block.vector
        def _(dve):
            def split_w(n):
                dve.wait_ge(w1_loaded, (n + 1) * 16)
                nc.vector.tensor_copy(w1_high[:, 0:2, :], w1t[:])
                nc.vector.tensor_scalar(w1_high[:, 2, :], w1t[:, 1, :], -1.0, None, ALU.mult).then_inc(w_high, 1)
                dve.wait_ge(w_high, n + 1)
                nc.vector.tensor_tensor(w1_rest[:, 0:2, :], w1t[:], w1_high[:, 0:2, :].bitcast(F32), ALU.subtract)
                nc.vector.scalar_tensor_tensor(w1_rest[:, 2, :], w1t[:, 1, :], -1.0,
                                               w1_high[:, 2, :].bitcast(F32), ALU.mult, ALU.subtract)
                dve.wait_ge(w2_loaded, (n + 1) * (16 * W2_DMAS))
                nc.vector.tensor_scalar(w2t[0:C, 0, :], w2t[0:C, 2, :], -1.0, None, ALU.mult).then_inc(w_ready, 1)

            def sums_of(k, part):
                m = len(CHUNKS[k])
                other = b_bank[2 * (k % 2) + (1 - part if k else 0)][0:C, 0:m * P]
                return xs[:, part, 0:m, :], other.rearrange("c (k m) -> c k m", k=m)[:, :, NCOS:P]

            def combine_negative(n, k):
                dve.wait_ge(b_copied, n * NCH + (k + 1))
                (r, from_im), (i, from_re) = sums_of(k, 0), sums_of(k, 1)
                if k == 0:
                    nc.vector.memset(i[:, :, 0:NCOS:HALF], 0.0)
                    nc.vector.tensor_scalar(i[:, :, NCOS:P], from_re, -1.0, None, ALU.mult).then_inc(combined, 1)
                    return
                nc.vector.tensor_tensor(r[:, :, NCOS:P], r[:, :, 1:HALF], from_im, ALU.add)
                nc.vector.tensor_tensor(i[:, :, NCOS:P], i[:, :, 1:HALF], from_re, ALU.subtract)

            def combine_positive_real(n, k):
                r, from_im = sums_of(k, 0)
                nc.vector.tensor_tensor(r[:, :, 1:HALF], r[:, :, 1:HALF], from_im, ALU.subtract)

            def combine_positive_imag(n, k):
                i, from_re = sums_of(k, 1)
                nc.vector.tensor_tensor(i[:, :, 1:HALF], i[:, :, 1:HALF], from_re, ALU.add).then_inc(combined, 1)

            def rest_x(n, k):
                dve.wait_ge(x_high, n * NCH + (k + 1))
                m = len(CHUNKS[k])
                nc.vector.tensor_tensor(rest[k % 2][0:C, :, 0:m * P],
                                        xs[:, :, 0:m, :].rearrange("c r k m -> c r (k m)"),
                                        high[k % 2][0:C, :, 0:m * P].bitcast(F32),
                                        ALU.subtract).then_inc(x_ready, 1)

            def shrink(n, k):
                for j, k0, m in BANKS_OF[k]:
                    dve.wait_ge(above_ready, n * (NB - 1) + (j + 1 if j == 0 else j))
                    if k >= TAIL and k0 == 0:
                        nc.vector.memset(unscaled(k)[1][:, 0:1], LEAST)
                    dst = z_place(k, k0, m)
                    nc.vector.scalar_tensor_tensor(dst, parts(j, m), LAMBDA, dst, ALU.add,
                                                   ALU.min).then_inc(z_ready, 1)

            def turn_real(n):
                dve.wait_ge(z_ready, n * NB + 1)
                nc.vector.tensor_scalar(real_z[:, 1, 1, :], real_z[:, 1, 1, :], -1.0, None,
                                        ALU.mult).then_inc(turned_real, 1)

            def copy_merged(n):
                dve.wait_ge(d_done, n * NB + (MERGED + 1))
                values, _ = unscaled(0)
                nc.vector.tensor_copy(values, parts(MERGED, 1)).then_inc(z_ready, 1)

            def find_largest(n, i):
                dve.wait_ge(z_ready, n * NB + (BANKS_OF[i][-1][0] + 1 if i else MERGED + 1))
                _, row = unscaled(i)
                nc.vector.tensor_reduce(largest[:, i:i + 1], row, AX.X, ALU.max,
                                        apply_absolute_value=True).then_inc(largest_ready, 1)

            def find_power(n, i):
                dve.wait_ge(top_ready, n * NS + (i + 1))
                nc.vector.tensor_scalar(power[:, i:i + 1].bitcast(I32), top[:, i:i + 1].bitcast(I32),
                                        EXPONENT_MASK, None, ALU.bitwise_and).then_inc(power_ready, 1)

            def find_scale(n, i):
                dve.wait_ge(power_ready, n * NS + (i + 1))
                nc.vector.tensor_scalar(scale[:, i:i + 1].bitcast(I32), power[:, i:i + 1].bitcast(I32),
                                        -1, SCALE_BITS, ALU.mult, ALU.add).then_inc(scale_ready, 1)

            def rest_z(n, i):
                dve.wait_ge(z_high, n * NS + (i + 1))
                values, _ = unscaled(i)
                hi, lo = z_slots(i, 0), z_slots(i, 1)
                for part in range(2):
                    last = nc.vector.scalar_tensor_tensor(
                        lo[:, part], values[:, part, :].rearrange("p (k c) -> p k c", c=C), scale[:, i:i + 1],
                        hi[:, part], ALU.mult, ALU.subtract)
                last.then_inc(z_split, 1)

            def double_z(n, i, last):
                dve.wait_ge(z_split, n * NS + (last + 1))
                ky, end = CHUNKS[i][0], (CHUNKS[last][-1] if last else 0) + 1
                nc.vector.tensor_copy(z_parts[:, P + ky:P + end, :, :],
                                      z_parts[:, ky:end, :, :]).then_inc(z_doubled, 1)

            def scales_by_slot(n):
                nc.vector.tensor_tensor(own[:], power[0:NS, :], diag[:], ALU.mult).then_inc(own_ready, 1)

            def take_scales(n):
                dve.wait_ge(picked, n + 1)
                nc.vector.tensor_reduce(back, slot_scales, AX.X, ALU.add).then_inc(back_ready, 1)
                dve.wait_ge(back_ready, n + 1)
                nc.vector.tensor_scalar(turned, sgn, back, None, ALU.mult).then_inc(turned_ready, 1)
                dve.wait_ge(turned_ready, n + 2)

            def combine_u(n, g):
                dve.wait_ge(e_copied, n * GROUPS + (g + 1))
                o = us[g % E_BANKS]
                sin = e_bank[g % E_BANKS].rearrange("p (c h) -> p c h", c=GC)[:, :, NCOS:P]
                nc.vector.scalar_tensor_tensor(o[:, :, P - 1:HALF:-1], sin, turned[:, 1:2], o[:, :, 1:HALF],
                                               ALU.mult, ALU.add)
                nc.vector.scalar_tensor_tensor(o[:, :, 1:HALF], sin, turned[:, 0:1], o[:, :, 1:HALF],
                                               ALU.mult, ALU.add).then_inc(combined_u, 1)

            def add_x(n, s, g):
                dve.wait_ge(f_done, n * GROUPS + (g + 1))
                dst = tile[s][:, :, g * GC:(g + 1) * GC].rearrange("p h c -> p c h")
                nc.vector.tensor_tensor(dst, dst, d_bank[g % 2].rearrange("p (c h) -> p c h", c=GC),
                                        ALU.add).then_inc(added, 1)

            for i in range(2):
                nc.vector.memset(o_r[i][C:C + 1, :, :], 1.0).then_inc(x_stored[i], 1)
            nc.vector.memset(started[:, 0:1], 0.0).then_inc(added, 1)
            nc.vector.memset(started[:, 1:2], 0.0).then_inc(w_ready, 1)
            dve.wait_ge(consts_in, 16 * CONSTANTS)
            nc.vector.tensor_copy(pick[:], picks)
            nc.vector.tensor_copy(gw_high[:], gw).then_inc(g_high, 1)
            dve.wait_ge(g_high, 1)
            nc.vector.tensor_tensor(gw_rest[:], gw, gw_high[:].bitcast(F32), ALU.subtract).then_inc(g_ready, 1)
            dve.wait_ge(g_ready, 1)
            nc.vector.memset(turned, 0.0).then_inc(turned_ready, 1)
            with dve.Fori(0, IMAGES * PAIRS) as t:
                for s in range(2):
                    n = t * 2 + s
                    split_w(n)
                    for k in range(-2, TAIL):
                        combine_negative(n, k + 2)
                        if k == 2:
                            find_power(n, 0)
                        if k >= 2:
                            find_power(n, k - 1)
                        if k + 2:
                            combine_positive_real(n, k + 2)
                        if k == 2:
                            find_scale(n, 0)
                        if k >= 2:
                            find_scale(n, k - 1)
                        if k + 2:
                            combine_positive_imag(n, k + 2)
                        if k == 2:
                            rest_z(n, 0)
                        if k >= 2:
                            rest_z(n, k - 1)
                        rest_x(n, k + 2)
                        if k == 2:
                            double_z(n, 0, 0)
                        if k >= 3:
                            double_z(n, k - 2, k - 2)
                        if k == 1:
                            copy_merged(n)
                            find_largest(n, 0)
                        if k >= 0:
                            shrink(n, k)
                        if k == 0:
                            turn_real(n)
                        if 1 <= k < TAIL - 1:
                            find_largest(n, k)
                    combine_negative(n, TAIL + 2)
                    combine_positive_real(n, TAIL + 2)
                    combine_positive_imag(n, TAIL + 2)
                    find_largest(n, TAIL - 1)
                    rest_x(n, TAIL + 2)
                    find_power(n, TAIL - 1)
                    find_scale(n, TAIL - 1)
                    double_z(n, TAIL - 2, TAIL - 2)
                    shrink(n, TAIL)
                    rest_z(n, TAIL - 1)
                    find_largest(n, TAIL)
                    double_z(n, TAIL - 1, TAIL - 1)
                    find_power(n, TAIL)
                    find_scale(n, TAIL)
                    shrink(n, TAIL + 1)
                    find_largest(n, TAIL + 1)
                    rest_z(n, TAIL)
                    find_power(n, TAIL + 1)
                    find_scale(n, TAIL + 1)
                    shrink(n, TAIL + 2)
                    find_largest(n, TAIL + 2)
                    rest_z(n, TAIL + 1)
                    find_power(n, TAIL + 2)
                    find_scale(n, TAIL + 2)
                    scales_by_slot(n)
                    double_z(n, TAIL, TAIL + 1)
                    rest_z(n, TAIL + 2)
                    double_z(n, TAIL + 2, TAIL + 2)
                    take_scales(n)
                    for g in range(GROUPS + E_BANKS - 1):
                        if g < GROUPS:
                            combine_u(n, g)
                        if g >= E_BANKS - 1:
                            add_x(n, s, g - E_BANKS + 1)


_INS = ["x", "L0_conv_w1", "L0_conv_b1", "L0_conv_w2", "L0_conv_b2"]


def _tables(p):
    import numpy as np
    half = p // 2
    angle = 2 * np.pi * (np.outer(np.arange(p), np.arange(half + 1)) % p) / p
    cos, sin = np.cos(angle), np.sin(angle)
    kx = np.concatenate([np.arange(half + 1), -np.arange(1, half)])
    f_x = np.concatenate([cos[:, :half + 1], -sin[:, 1:half]], 1)
    back = 2 * np.pi * (np.outer(kx, np.arange(half + 1)) % p) / p
    g_h = np.concatenate([np.cos(back), np.sin(back)[:, 1:half]], 1)
    g_h_high = g_h.astype(np.float16)
    g_h_rest = (g_h - g_h_high).astype(np.float16)
    g_w = 2 * f_x.T / p ** 2
    g_w[0] /= 2
    g_w[half] /= 2
    partner = np.array([list(kx % p).index((-k) % p) for k in kx])
    same, swap = np.eye(p), np.eye(p)[partner]
    even, odd = (same + swap) / 2, (same - swap) / 2
    mirror = np.stack([even, odd.T], 1)
    turn = np.ones((p, 2))
    turn[:half, 0] = -1
    turn[half:, 1] = -1
    group = np.array([(k % half + 3) // 4 for k in range(p)])
    chunk_of_slot = (group[None, :] == np.arange(half // 4 + 1)[:, None])
    diagonal = np.eye(half // 4 + 1) * 2.0 ** -14
    out = {k: np.ascontiguousarray(v, np.float32) for k, v in
           dict(f_x=f_x, g_h_high=g_h_high, g_h_rest=g_h_rest, g_w=g_w, mirror=mirror, turn=turn,
                chunk_of_slot=chunk_of_slot, diagonal=diagonal).items()}
    out["g_h_high"], out["g_h_rest"] = g_h_high, g_h_rest
    return out


def kernel(**inputs):
    import numpy as _np
    import concourse.bacc as _bacc
    from concourse import mybir as _mybir
    from concourse.bass_utils import run_bass_kernel_spmd as _run

    nc = _bacc.Bacc("TRN2", target_bir_lowering=False, num_devices=1)
    arrays, args = {}, []
    for name in _INS:
        arrays[f"in_{name}_dram"] = _np.ascontiguousarray(inputs[name])
    for name, a in _tables(128).items():
        arrays[f"const_{name}_dram"] = a
    for name, a in arrays.items():
        args.append(nc.dram_tensor(name, a.shape, _mybir.dt.from_np(a.dtype), kind="ExternalInput").ap())
    shape = inputs["x"].shape
    args.append(nc.dram_tensor("out_0_dram", shape, _mybir.dt.float32, kind="ExternalOutput").ap())
    fourier_mixer_kernel(nc, *args)
    r = _run(nc, [arrays], core_ids=[0])
    return r.results[0]["out_0_dram"]
```
